# Optimizing a Trainium2 kernel written in Bass

```python
import numpy as np
import jax
import jax.numpy as jnp

def _softmax(x, axis=-1):
    return jax.nn.softmax(x, axis=axis)

def _gelu(x):
    return jax.nn.gelu(x, approximate=True)

def _silu(x):
    return jax.nn.silu(x)

def _sigmoid(x):
    return jax.nn.sigmoid(x)

def _layernorm(x, axis=-1, eps=1e-05):
    m = jnp.mean(x, axis=axis, keepdims=True)
    v = jnp.var(x, axis=axis, keepdims=True)
    return (x - m) / jnp.sqrt(v + eps)

def _scatter_add(tgt, idx, src, axis=0):
    return tgt.at[idx].add(src)

def _segment_sum(src, seg, n):
    return jax.ops.segment_sum(src, seg, n)
kernel_name = 'mk_seq_preln_d1_jaxref_r8_612a7e'

def setup_inputs(seed: int=0):
    np.random.seed(seed)
    _w = jnp.asarray

    def _L0_attn_setup():
        import jax, jax.numpy as jnp
        import numpy as np
        B, S, D, H = (1, 512, 128, 16)
        DH = D // H

        def _positional_encoding(seq_len, d_model, dtype):
            pos = jnp.arange(seq_len, dtype=dtype)[:, None]
            div = jnp.exp(jnp.arange(0, d_model, 2, dtype=dtype) * (-np.log(10000.0) / d_model))
            pe = jnp.zeros((seq_len, d_model), dtype=dtype)
            pe = pe.at[:, 0::2].set(jnp.sin(pos * div))
            pe = pe.at[:, 1::2].set(jnp.cos(pos * div))
            return pe
        key = jax.random.key(seed)
        ks = jax.random.split(key, 11)
        s = 1.0 / np.sqrt(D)
        return {'x': jax.random.normal(ks[0], (B, S, D), dtype=jnp.float32), 'Wq': jax.random.normal(ks[1], (D, D), dtype=jnp.float32) * s, 'bq': jnp.zeros((D,), dtype=jnp.float32), 'Wk': jax.random.normal(ks[2], (D, D), dtype=jnp.float32) * s, 'bk': jnp.zeros((D,), dtype=jnp.float32), 'Wv': jax.random.normal(ks[3], (D, D), dtype=jnp.float32) * s, 'bv': jnp.zeros((D,), dtype=jnp.float32), 'Wo': jax.random.normal(ks[4], (D, D), dtype=jnp.float32) * s, 'bo': jnp.zeros((D,), dtype=jnp.float32), 'gamma': jnp.ones((D,), dtype=jnp.float32), 'beta': jnp.zeros((D,), dtype=jnp.float32)}
    _L0_attn_in = _L0_attn_setup()

    def _L0_ffn_setup():
        import jax, jax.numpy as jnp
        import numpy as np
        E = 32
        H = 128
        I = 64
        G = 8
        TKG = 4
        TOPK = 8
        NSH = 2
        SCALE = 2.5
        key = jax.random.key(seed)
        ks = jax.random.split(key, 10)
        s = 0.02
        return {'hidden_states': jax.random.normal(ks[0], (2, 128, H), jnp.float32), 'gate_w': jax.random.normal(ks[1], (E, H), jnp.float32) * s, 'gate_bias': jax.random.normal(ks[2], (E,), jnp.float32) * s, 'w_gate': jax.random.normal(ks[3], (E, I, H), jnp.float32) * s, 'w_up': jax.random.normal(ks[4], (E, I, H), jnp.float32) * s, 'w_down': jax.random.normal(ks[5], (E, H, I), jnp.float32) * s, 'sh_gate': jax.random.normal(ks[6], (I * NSH, H), jnp.float32) * s, 'sh_up': jax.random.normal(ks[7], (I * NSH, H), jnp.float32) * s, 'sh_down': jax.random.normal(ks[8], (H, I * NSH), jnp.float32) * s}
    _L0_ffn_in = _L0_ffn_setup()
    _d = {'L0_attn_x': _L0_attn_in['x'], 'L0_attn_Wq': _L0_attn_in['Wq'], 'L0_attn_bq': _L0_attn_in['bq'], 'L0_attn_Wk': _L0_attn_in['Wk'], 'L0_attn_bk': _L0_attn_in['bk'], 'L0_attn_Wv': _L0_attn_in['Wv'], 'L0_attn_bv': _L0_attn_in['bv'], 'L0_attn_Wo': _L0_attn_in['Wo'], 'L0_attn_bo': _L0_attn_in['bo'], 'L0_attn_gamma': _L0_attn_in['gamma'], 'L0_attn_beta': _L0_attn_in['beta'], 'L0_ffn_gate_w': _L0_ffn_in['gate_w'], 'L0_ffn_gate_bias': _L0_ffn_in['gate_bias'], 'L0_ffn_w_gate': _L0_ffn_in['w_gate'], 'L0_ffn_w_up': _L0_ffn_in['w_up'], 'L0_ffn_w_down': _L0_ffn_in['w_down'], 'L0_ffn_sh_gate': _L0_ffn_in['sh_gate'], 'L0_ffn_sh_up': _L0_ffn_in['sh_up'], 'L0_ffn_sh_down': _L0_ffn_in['sh_down']}
    _x0 = _d['L0_attn_x']
    _d['L0_attn_x'] = jax.random.normal(jax.random.fold_in(jax.random.key(seed), 1), (8, 512, 128), dtype=_x0.dtype)
    del _x0
    return _d

def reference(L0_attn_x, L0_attn_Wq, L0_attn_bq, L0_attn_Wk, L0_attn_bk, L0_attn_Wv, L0_attn_bv, L0_attn_Wo, L0_attn_bo, L0_attn_gamma, L0_attn_beta, L0_ffn_gate_w, L0_ffn_gate_bias, L0_ffn_w_gate, L0_ffn_w_up, L0_ffn_w_down, L0_ffn_sh_gate, L0_ffn_sh_up, L0_ffn_sh_down):

    def _L0_attn_ref(x, Wq, bq, Wk, bk, Wv, bv, Wo, bo, gamma, beta):
        import jax, jax.numpy as jnp
        import numpy as np
        B, S, D, H = (1, 512, 128, 16)
        DH = D // H

        def _positional_encoding(seq_len, d_model, dtype):
            pos = jnp.arange(seq_len, dtype=dtype)[:, None]
            div = jnp.exp(jnp.arange(0, d_model, 2, dtype=dtype) * (-np.log(10000.0) / d_model))
            pe = jnp.zeros((seq_len, d_model), dtype=dtype)
            pe = pe.at[:, 0::2].set(jnp.sin(pos * div))
            pe = pe.at[:, 1::2].set(jnp.cos(pos * div))
            return pe
        b, s, d = x.shape
        h = x + _positional_encoding(s, d, x.dtype)[None, :, :]
        q = (h @ Wq + bq).reshape(b, s, H, DH)
        k = (h @ Wk + bk).reshape(b, s, H, DH)
        v = (h @ Wv + bv).reshape(b, s, H, DH)
        scores = jnp.einsum('bshd,bthd->bhst', q, k) / np.sqrt(DH)
        attn = jax.nn.softmax(scores, axis=-1)
        out = jnp.einsum('bhst,bthd->bshd', attn, v).reshape(b, s, d)
        out = out @ Wo + bo
        y = h + out
        mu = jnp.mean(y, axis=-1, keepdims=True)
        var = jnp.var(y, axis=-1, keepdims=True)
        return (y - mu) * jax.lax.rsqrt(var + 1e-05) * gamma + beta

    def _L0_ffn_ref(hidden_states, gate_w, gate_bias, w_gate, w_up, w_down, sh_gate, sh_up, sh_down):
        import jax, jax.numpy as jnp
        import numpy as np
        E = 32
        H = 128
        I = 64
        G = 8
        TKG = 4
        TOPK = 8
        NSH = 2
        SCALE = 2.5
        B, S, Hd = hidden_states.shape
        h = hidden_states.reshape(-1, Hd)
        logits = h.astype(jnp.float32) @ gate_w.T
        scores = jax.nn.sigmoid(logits)
        sc = scores + gate_bias
        grp = sc.reshape(-1, G, E // G)
        group_scores = jax.lax.top_k(grp, 2)[0].sum(-1)
        gidx = jax.lax.top_k(group_scores, TKG)[1]
        gmask = jnp.sum(jax.nn.one_hot(gidx, G, dtype=sc.dtype), axis=1)
        smask = jnp.repeat(gmask, E // G, axis=1)
        masked = jnp.where(smask > 0, sc, jnp.zeros_like(sc))
        tki = jax.lax.top_k(masked, TOPK)[1]
        tkw = jnp.take_along_axis(scores, tki, axis=1)
        tkw = tkw / (tkw.sum(-1, keepdims=True) + 1e-20)
        tkw = tkw * SCALE
        combine = (jax.nn.one_hot(tki, E, dtype=tkw.dtype) * tkw[..., None]).sum(1)
        g = jax.nn.silu(jnp.einsum('th,eih->tei', h, w_gate))
        u = jnp.einsum('th,eih->tei', h, w_up)
        routed = jnp.einsum('tei,ehi->th', g * u * combine[:, :, None], w_down)
        sg = jax.nn.silu(h @ sh_gate.T)
        shared = sg * (h @ sh_up.T) @ sh_down.T
        return (routed + shared).reshape(B, S, Hd)
    x = L0_attn_x
    x = x + _L0_attn_ref(_layernorm(x, axis=-1), L0_attn_Wq, L0_attn_bq, L0_attn_Wk, L0_attn_bk, L0_attn_Wv, L0_attn_bv, L0_attn_Wo, L0_attn_bo, L0_attn_gamma, L0_attn_beta)
    x = x + _L0_ffn_ref(_layernorm(x, axis=-1), L0_ffn_gate_w, L0_ffn_gate_bias, L0_ffn_w_gate, L0_ffn_w_up, L0_ffn_w_down, L0_ffn_sh_gate, L0_ffn_sh_up, L0_ffn_sh_down)
    return x

_drawn_inputs = setup_inputs


def setup_inputs(seed=0):
    import zlib

    import numpy as np

    out = dict(_drawn_inputs(seed))
    spreads = {'L0_attn_bq': (0.0, 0.8),
     'L0_attn_bk': (0.0, 0.8),
     'L0_attn_bv': (0.0, 0.1),
     'L0_attn_bo': (0.0, 0.1),
     'L0_attn_gamma': (1.0, 0.2),
     'L0_attn_beta': (0.0, 0.1)}
    factors = {'L0_ffn_gate_w': 8.0,
     'L0_ffn_gate_bias': 8.0,
     'L0_ffn_w_gate': 8.0,
     'L0_ffn_w_up': 8.0,
     'L0_ffn_w_down': 8.0,
     'L0_ffn_sh_gate': 8.0,
     'L0_ffn_sh_up': 8.0,
     'L0_ffn_sh_down': 8.0}
    for name, (base, spread) in spreads.items():
        noise = np.random.default_rng([zlib.crc32(name.encode()), seed]).standard_normal(out[name].shape)
        drawn = base * np.exp(spread * noise) if base else spread * noise
        out[name] = jnp.asarray(drawn.astype(out[name].dtype))
    for name, factor in factors.items():
        out[name] = (out[name] * factor).astype(out[name].dtype)
    return out
```

```python
from contextlib import ExitStack

import concourse.bass as bass
from concourse import mybir

F32 = mybir.dt.float32
F32R = mybir.dt.float32r
ALU = mybir.AluOpType
ACT = mybir.ActivationFunctionType
AX_X = mybir.AxisListType.X

P = 128
B = 8
T = 512
TT = T // P
H = 16
DH = P // H
GROUPS = 4
E = 32
EG = 8
EI = 64
BLOCKS = 1 + E * EI // P
STACK = 3 * DH
UNITS = H * TT
SETS = UNITS // 4
SLOTS = 16
CHUNKS = 4
EPS = 1e-5
ROUTE_SCALE = 2.5
ROUTE_STEPS = 16
LN1, LN2, LN3 = range(3)

MAX_SETS = [0, 0, 0, 2, 2, 2, 2, 2, 2, 1, 1, 1, 1, 0, 0, 0]
FFN_SLOTS = [[(7 + s, 2)] for s in range(10)] + [[(s, 1)] for s in range(5)] + [[(5, 1), (6, 1)]]


class Count:

    def __init__(self, trip, scale, base):
        self.trip, self.scale, self.base = trip, scale, base

    def __add__(self, k):
        return Count(self.trip, self.scale, self.base + k)

    def __sub__(self, k):
        return self + -k

    def __mul__(self, k):
        return Count(self.trip, self.scale * k, self.base * k)

    __rmul__ = __mul__


def at(count):
    return count.trip * count.scale + count.base if isinstance(count, Count) else count


class Batch:

    def __init__(self, first, trip=None):
        self.first, self.trip, self.par = first, trip, first % 2
        self.n = first if trip is None else Count(trip, 2, first)
        self.pair = first // 2 if trip is None else Count(trip, 1, first // 2)
        self.exists = 0 <= first < B

    def plus(self, k):
        return Batch(self.first + k, self.trip)


def wait(eng, sem, count):
    if isinstance(count, Count) or count > 0:
        eng.wait_ge(sem, at(count))


def build_layer(nc, x, wq, wk, wv, wo, bq, bk, bv, bo, gamma, beta, gate_wT, gate_bias, w_gateT,
                w_upT, w_downT, pe_table, identity, tie_mask, out):
    with ExitStack() as ctx:
        def sb(name, shape, dt=F32):
            return ctx.enter_context(nc.sbuf_tensor(name, shape, dt))

        def ps(name, shape):
            return ctx.enter_context(nc.psum_tensor(name, shape, F32))

        def sem(name):
            return ctx.enter_context(nc.semaphore(name))

        ident = sb("ident", [P, P])
        ties = sb("ties", [P, EG, EG])
        pos = sb("pos", [P, TT, P])
        w_hi = sb("w_hi", [P, 4, P], F32R)
        w_lo = sb("w_lo", [P, 4, P], F32R)
        gate_raw = sb("gate_raw", [P, E])
        gate_hi = sb("gate_hi", [P, E], F32R)
        gate_lo = sb("gate_lo", [P, E], F32R)
        wgu_hi = sb("wgu_hi", [P, 2, BLOCKS, P], F32R)
        wgu_lo = sb("wgu_lo", [P, 2, BLOCKS, P], F32R)
        w_down = sb("w_down", [P, BLOCKS, P])
        qk_bias = sb("qk_bias", [P, 2])
        bv_row = sb("bv_row", [P, P])
        bo_row = sb("bo_row", [P, P])
        gamma_row = sb("gamma_row", [P, P])
        beta_row = sb("beta_row", [P, P])
        route_bias = sb("route_bias", [P, E])
        minus_half = sb("minus_half", [P, TT])

        x_in = sb("x_in", [P, 2, TT, P])
        x_beta = sb("x_beta", [P, 2, TT, P])
        xn = sb("xn", [P, TT, P])
        h = sb("h", [P, TT, P])
        h_bo = sb("h_bo", [P, 2, TT, P])
        hT_hi = sb("hT_hi", [P, T], F32R)
        hT_lo = sb("hT_lo", [P, T], F32R)
        qk_hi = sb("qk_hi", [P, 2, T], F32R)
        qk_lo = sb("qk_lo", [P, 2, T], F32R)
        q_stack = [sb(f"q_stack{i}", [P, GROUPS, T], F32R) for i in range(2)]
        k_stack = [sb(f"k_stack{i}", [P, GROUPS, T], F32R) for i in range(2)]
        values = [sb(f"values{i}", [P, TT, H, DH + 1]) for i in range(2)]
        neg_max = sb("neg_max", [P, TT, 4, GROUPS])
        max_parts = sb("max_parts", [P, TT, 4, 2, GROUPS])
        maxT = sb("maxT", [4 * 2 * GROUPS, T])
        probs = sb("probs", [P, 8, T])
        oT = sb("oT", [P, 2, T])
        o_rcp = sb("o_rcp", [P, 2, TT, 4])
        o = sb("o", [P, TT, P])
        o2T_hi = sb("o2T_hi", [P, T], F32R)
        o2T_lo = sb("o2T_lo", [P, T], F32R)
        y = sb("y", [P, TT, P])
        x2 = sb("x2", [P, 2, TT, P])
        xn2T_hi = sb("xn2T_hi", [P, 2, T], F32R)
        xn2T_lo = sb("xn2T_lo", [P, 2, T], F32R)
        stats = sb("stats", [P, 3, TT, 6])
        moments = sb("moments", [P, 3, TT, 2])
        var_eps = sb("var_eps", [P, 3, TT])
        rstd = sb("rstd", [P, 3, TT])
        r_exp = sb("r_exp", [P, TT, E])
        r_den = sb("r_den", [P, TT, E])
        r_sig = sb("r_sig", [P, TT, E])
        r_sc = sb("r_sc", [P, TT, E])
        r_max = sb("r_max", [P, TT * EG, 2])
        r_min = sb("r_min", [P, TT * EG, 2])
        r_own = sb("r_own", [P, TT * EG, 2])
        r_two = sb("r_two", [P, TT * EG, 2])
        r_grp = sb("r_grp", [P, TT, EG])
        r_gt = sb("r_gt", [P, TT, EG, EG])
        r_eq = sb("r_eq", [P, TT, EG, EG])
        r_rank = sb("r_rank", [P, TT, EG])
        r_open = sb("r_open", [P, TT, EG])
        r_masked = sb("r_masked", [P, TT, E])
        r_top = sb("r_top", [P, TT, 8])
        r_rest = sb("r_rest", [P, TT, E])
        r_sel = sb("r_sel", [P, TT, E])
        r_w = sb("r_w", [P, TT, E])
        r_sum = sb("r_sum", [P, 3, TT])
        comb = sb("comb", [P, TT, E])
        combT = sb("combT", [E, T])
        comb_all = sb("comb_all", [P, 8, T])
        f_tanh = sb("f_tanh", [P, 2, T])
        f_silu = sb("f_silu", [P, 2, T])
        f_prod = sb("f_prod", [P, 3, T])
        f_act = sb("f_act", [P, 3, T])
        ffnT = sb("ffnT", [P, T])

        max_bank = ps("max_bank", [P, 2, T])
        exp_bank = ps("exp_bank", [P, 2, T])
        out_bank = ps("out_bank", [P, T])
        down_bank = ps("down_bank", [P, T])
        shared = ps("shared", [P, 2, T])

        w_raw = y
        raw_experts = [comb_all[:].rearrange("p a b -> p (a b)")[:, 0:BLOCKS * P],
                       probs[:].rearrange("p a b -> p (a b)")[:, 0:BLOCKS * P]]

        qk_scratch = nc.dram_tensor("qk_scratch", (2, 2, 2, P, T), F32).ap()
        max_scratch = nc.dram_tensor("max_scratch", (2, 4 * 2 * GROUPS, T), F32).ap()
        comb_scratch = nc.dram_tensor("comb_scratch", (2, E, T), F32).ap()

        consts_loaded = sem("consts_loaded")
        weights_loaded = sem("weights_loaded")
        experts_loaded = sem("experts_loaded")
        down_loaded = sem("down_loaded")
        ones_set = sem("ones_set")
        values_set = sem("values_set")
        out_bank_set = sem("out_bank_set")
        h_bo_ready = sem("h_bo_ready")
        comb_step = sem("comb_step")
        exponent_set = sem("exponent_set")
        w_hi_ready = sem("w_hi_ready")
        w_split = sem("w_split")
        experts_hi = sem("experts_hi")
        experts_split = sem("experts_split")
        x_loaded = [sem(f"x_loaded{i}") for i in range(2)]
        ln_step = [sem(f"ln_step{i}") for i in range(3)]
        var_ready = [sem(f"var_ready{i}") for i in range(3)]
        rstd_ready = [sem(f"rstd_ready{i}") for i in range(3)]
        xn_ready = sem("xn_ready")
        h_ready = sem("h_ready")
        x_beta_ready = sem("x_beta_ready")
        hT_ready = sem("hT_ready")
        hT_hi_ready = sem("hT_hi_ready")
        hT_split = sem("hT_split")
        qk_ready = sem("qk_ready")
        qk_hi_ready = sem("qk_hi_ready")
        qk_lo_ready = sem("qk_lo_ready")
        qk_stored = sem("qk_stored")
        stack_loaded = sem("stack_loaded")
        v_ready = sem("v_ready")
        values_ready = sem("values_ready")
        max_scores = sem("max_scores")
        max_taken = sem("max_taken")
        max_hi = sem("max_hi")
        max_split = sem("max_split")
        maxT_ready = sem("maxT_ready")
        maxT_copied = sem("maxT_copied")
        max_stored = sem("max_stored")
        max_loaded = sem("max_loaded")
        scores_ready = sem("scores_ready")
        exp_done = sem("exp_done")
        pv_done = sem("pv_done")
        oT_copied = sem("oT_copied")
        oq_ready = sem("oq_ready")
        o_rcp_ready = sem("o_rcp_ready")
        o_ready = sem("o_ready")
        o2T_ready = sem("o2T_ready")
        o2T_hi_ready = sem("o2T_hi_ready")
        o2T_split = sem("o2T_split")
        wo_ready = sem("wo_ready")
        y_ready = sem("y_ready")
        yn_ready = sem("yn_ready")
        x2_step = sem("x2_step")
        xn2_ready = sem("xn2_ready")
        xn2T_ready = sem("xn2T_ready")
        xn2T_hi_ready = sem("xn2T_hi_ready")
        xn2T_split = sem("xn2T_split")
        logits_ready = sem("logits_ready")
        logits_exp = sem("logits_exp")
        route_step = sem("route_step")
        comb_ready = sem("comb_ready")
        combT_ready = sem("combT_ready")
        combT_copied = sem("combT_copied")
        comb_stored = sem("comb_stored")
        comb_loaded = [sem(f"comb_loaded{i}") for i in range(CHUNKS)]
        gate_ready = sem("gate_ready")
        up_ready = sem("up_ready")
        tanh_done = sem("tanh_done")
        silu_done = sem("silu_done")
        prod_done = sem("prod_done")
        act_done = sem("act_done")
        down_done = sem("down_done")
        ffnT_copied = sem("ffnT_copied")
        ffn_ready = sem("ffn_ready")
        result_ready = sem("result_ready")
        result_stored = sem("result_stored")

        x_view = x.rearrange("b (t p) d -> b p t d", p=P)
        out_view = out.rearrange("b (t p) d -> b p t d", p=P)
        N_CONSTS = 16 * 11
        LOOP_FROM, LOOP_TRIPS = 2, 2

        def run_iterations(eng, iteration, start_loop=None, end_loop=None):
            for t in range(LOOP_FROM):
                iteration(Batch(t))
            with eng.Fori(0, LOOP_TRIPS) as trip:
                eng.get_value_cache().nocache = True
                if start_loop:
                    start_loop(Batch(LOOP_FROM, trip))
                for u in range(2):
                    iteration(Batch(LOOP_FROM + u, trip))
            if end_loop:
                end_loop(Batch(LOOP_FROM + 2 * LOOP_TRIPS))
            for t in range(LOOP_FROM + 2 * LOOP_TRIPS, B + 2):
                iteration(Batch(t))

        block = ctx.enter_context(nc.Block())

        @block.sync
        def _(sp):
            def load_x(n):
                if n.first >= 2:
                    sp.wait_ge(xn_ready, at(n.plus(-2).n + 1))
                    sp.wait_ge(x_beta_ready, at(n.plus(-2).n + 1))
                sp.dma_start(x_in[:, n.par], x_view[at(n.n)]).then_inc(x_loaded[n.par], 16)

            def stack_qk(n):
                for side in range(2):
                    sp.wait_ge(qk_hi_ready, at(2 * n.n + side + 1))
                    sp.dma_start(qk_scratch[n.par, side, 0], qk_hi[:, side].bitcast(F32)).then_inc(qk_stored, 16)
                    sp.wait_ge(qk_lo_ready, at(2 * n.n + side + 1))
                    sp.dma_start(qk_scratch[n.par, side, 1], qk_lo[:, side].bitcast(F32)).then_inc(qk_stored, 16)
                sp.wait_ge(qk_stored, at(64 * n.n + 64))
                wait(sp, scores_ready, UNITS * (n.n - 1))
                for side, stack, parts in ((0, q_stack, (0, 0, 1)), (1, k_stack, (0, 1, 0))):
                    for j, part in enumerate(parts):
                        rows = qk_scratch[n.par, side, part].rearrange("(i g d) n -> i d g n", g=GROUPS, d=DH)
                        for i in range(4):
                            row = 32 * i + DH * j
                            sp.dma_start(stack[n.par][row:row + DH].bitcast(F32), rows[i]).then_inc(stack_loaded, 16)

            def stack_max(n):
                sp.wait_ge(maxT_copied, at(n.n + 1))
                sp.dma_start(max_scratch[n.par], maxT[:]).then_inc(max_stored, 16)
                sp.wait_ge(max_stored, at(16 * n.n + 16))
                rows = max_scratch[n.par].rearrange("(i a g) n -> i a g n", a=2, g=GROUPS)
                for i in range(4):
                    row = 32 * i + STACK
                    sp.dma_start(q_stack[n.par][row:row + 2].bitcast(F32), rows[i]).then_inc(max_loaded, 16)

            def store_comb(f):
                sp.wait_ge(combT_copied, at(f.n + 1))
                sp.dma_start(comb_scratch[f.par], combT[:]).then_inc(comb_stored, 16)
                sp.wait_ge(comb_stored, at(16 * f.n + 16))

            def broadcast_comb(f, c):
                rows = comb_scratch[f.par].rearrange("(k a) n -> a k n", a=2)
                wait(sp, act_done, (BLOCKS - 1) * f.n + 4 * (c - 2) + 4)
                slot = 4 * (c % 2)
                for a in range(2):
                    src = rows[a, 4 * c:4 * c + 4].unsqueeze(0).broadcast_to([EI, 4, T])
                    sp.dma_start(comb_all[EI * a:EI * a + EI, slot:slot + 4], src).then_inc(comb_loaded[c], 16)

            def store_result(f):
                sp.wait_ge(result_ready, at(f.n + 1))
                sp.dma_start(out_view[at(f.n)], x2[:, f.par]).then_inc(result_stored, 16)

            load_x(Batch(0))
            for dst, src in ((ident[:], identity), (pos[:], pe_table), (ties[:], tie_mask),
                             (bv_row[:], bv.partition_broadcast(P)), (bo_row[:], bo.partition_broadcast(P)),
                             (gamma_row[:], gamma.partition_broadcast(P)),
                             (beta_row[:], beta.partition_broadcast(P)),
                             (route_bias[:], gate_bias.partition_broadcast(P)),
                             (gate_raw[:], gate_wT), (qk_bias[:, 0:1], bq.unsqueeze(1)),
                             (qk_bias[:, 1:2], bk.unsqueeze(1))):
                sp.dma_start(dst, src).then_inc(consts_loaded, 16)
            for n, w in enumerate((wq, wk, wv, wo)):
                sp.dma_start(w_raw[:, n], w).then_inc(weights_loaded, 16)
            load_x(Batch(1))
            for side, w in enumerate((w_gateT, w_upT)):
                sp.dma_start(raw_experts[side], w).then_inc(experts_loaded, 16)
            sp.dma_start(w_down[:], w_downT).then_inc(down_loaded, 16)
            sp.wait_ge(ones_set, 2)
            stack_qk(Batch(0))
            stack_max(Batch(0))

            def iteration(t):
                if t.plus(2).exists:
                    load_x(t.plus(2))
                if t.plus(1).exists:
                    stack_qk(t.plus(1))
                if t.plus(-2).exists:
                    broadcast_comb(t.plus(-2), 3)
                if t.plus(-1).exists:
                    if t.first == 1:
                        sp.wait_ge(experts_split, 2)
                    store_comb(t.plus(-1))
                    broadcast_comb(t.plus(-1), 0)
                    broadcast_comb(t.plus(-1), 1)
                if t.plus(-2).exists:
                    store_result(t.plus(-2))
                if t.plus(1).exists:
                    stack_max(t.plus(1))
                if t.plus(-1).exists:
                    broadcast_comb(t.plus(-1), 2)

            run_iterations(sp, iteration)
            sp.wait_ge(result_stored, 16 * B)

        @block.tensor
        def _(pe):
            last_reader = [None, None]

            def claim(bank, done, value):
                if last_reader[bank]:
                    done_before, value_before = last_reader[bank]
                    pe.wait_ge(done_before, at(value_before))
                last_reader[bank] = (done, value)

            def products(dst, pairs, start=True, stop=True):
                for n, (left, right) in enumerate(pairs):
                    last = nc.tensor.matmul(dst, left, right, start=start and n == 0,
                                            stop=stop and n == len(pairs) - 1)
                return last

            def transpose_h(n):
                pe.wait_ge(h_ready, at(n.n + 1))
                claim(0, hT_split, n.n + 1)
                for tt in range(TT):
                    last = nc.tensor.transpose(shared[:, 0, tt * P:tt * P + P], h[:, tt], ident[:])
                last.then_inc(hT_ready, 1)

            def project_qk(n):
                pe.wait_ge(hT_split, at(n.n + 1))
                for side in range(2):
                    bank = 1 - side
                    claim(bank, qk_lo_ready, 2 * n.n + side + 1)
                    products(shared[:, bank], [(w_hi[:, side], hT_hi[:]), (w_lo[:, side], hT_hi[:]),
                                               (w_hi[:, side], hT_lo[:])]).then_inc(qk_ready, 1)

            def project_v(n):
                claim(1, values_ready, n.n + 1)
                for tt in range(TT):
                    cols = slice(tt * P, tt * P + P)
                    last = products(shared[:, 1, cols], [(hT_hi[:, cols], w_hi[:, 2]), (hT_hi[:, cols], w_lo[:, 2]),
                                                         (hT_lo[:, cols], w_hi[:, 2])])
                last.then_inc(v_ready, 1)

            def max_unit(n, u):
                g, qt, i = u // (4 * TT), (u // 4) % TT, u % 4
                if u == 0:
                    pe.wait_ge(stack_loaded, at(16 * 24 * (n.n + 1)))
                wait(pe, max_taken, UNITS * n.n + u - 1)
                rows = slice(32 * i, 32 * i + STACK)
                nc.tensor.matmul(max_bank[:, u % 2], q_stack[n.par][rows, g, qt * P:qt * P + P],
                                 k_stack[n.par][rows, g, :], start=True, stop=True).then_inc(max_scores, 1)

            def transpose_max(n):
                pe.wait_ge(max_split, at(n.n + 1))
                claim(0, maxT_copied, n.n + 1)
                for tt in range(TT):
                    last = nc.tensor.transpose(shared[0:32, 0, tt * P:tt * P + P],
                                               max_parts[:, tt].rearrange("p i a g -> p (i a g)"), ident[:])
                last.then_inc(maxT_ready, 1)

            def exp_unit(b, u):
                g, kt, i = u // (4 * TT), (u // 4) % TT, u % 4
                if u == 0:
                    pe.wait_ge(max_loaded, at(64 * (b.n + 1)))
                wait(pe, exp_done, UNITS * b.n + u - 1)
                rows = slice(32 * i, 32 * i + STACK + 2)
                nc.tensor.matmul(exp_bank[:, u % 2], k_stack[b.par][rows, g, kt * P:kt * P + P],
                                 q_stack[b.par][rows, g, :], start=True, stop=True).then_inc(scores_ready, 1)

            def value_set(b, s):
                g, kt = s // TT, s % TT
                if s == 0:
                    pe.wait_ge(values_ready, at(b.n + 1))
                if s == 0 and b.first == 0:
                    pe.wait_ge(out_bank_set, 1)
                if kt == 0:
                    wait(pe, oT_copied, GROUPS * b.n + g)
                pe.wait_ge(exp_done, at(UNITS * b.n + 4 * s + 4))
                for i in range(4):
                    last = nc.tensor.matmul(out_bank[32 * i:32 * i + DH + 1], values[b.par][:, kt, 4 * i + g, :],
                                            probs[:, (4 * s + i) % 8], start=(kt == 0), stop=(kt == TT - 1))
                last.then_inc(pv_done, 1)

            def transpose_o(b, g):
                pe.wait_ge(oT_copied, at(GROUPS * b.n + g + 1))
                claim(1, o_ready, GROUPS * b.n + g + 1)
                for tt in range(TT):
                    cols = slice(tt * P, tt * P + P)
                    last = nc.tensor.transpose(shared[:, 1, cols], oT[:, g % 2, cols], ident[:])
                last.then_inc(oq_ready, 1)

            def transpose_o2(b):
                pe.wait_ge(o_ready, at(GROUPS * (b.n + 1)))
                claim(0, o2T_split, b.n + 1)
                for tt in range(TT):
                    last = nc.tensor.transpose(shared[:, 0, tt * P:tt * P + P], o[:, tt], ident[:])
                last.then_inc(o2T_ready, 1)

            def project_o(b):
                pe.wait_ge(o2T_split, at(b.n + 1))
                claim(1, y_ready, b.n + 1)
                for tt in range(TT):
                    cols = slice(tt * P, tt * P + P)
                    last = products(shared[:, 1, cols], [(o2T_hi[:, cols], w_hi[:, 3]), (o2T_hi[:, cols], w_lo[:, 3]),
                                                         (o2T_lo[:, cols], w_hi[:, 3])])
                last.then_inc(wo_ready, 1)

            def transpose_xn2(b):
                pe.wait_ge(xn2_ready, at(b.n + 1))
                claim(0, xn2T_split, b.n + 1)
                for tt in range(TT):
                    last = nc.tensor.transpose(shared[:, 0, tt * P:tt * P + P], y[:, tt], ident[:])
                last.then_inc(xn2T_ready, 1)

            def route(b):
                pe.wait_ge(xn2T_split, at(b.n + 1))
                claim(1, logits_exp, b.n + 1)
                hi, lo = xn2T_hi[:, b.par], xn2T_lo[:, b.par]
                for tt in range(TT):
                    cols = slice(tt * P, tt * P + P)
                    last = products(shared[:, 1, tt * E:tt * E + E], [(hi[:, cols], gate_hi[:]), (hi[:, cols], gate_lo[:]),
                                                                      (lo[:, cols], gate_hi[:])])
                last.then_inc(logits_ready, 1)

            def transpose_comb(b):
                pe.wait_ge(comb_ready, at(b.n + 1))
                claim(0, combT_copied, b.n + 1)
                for tt in range(TT):
                    last = nc.tensor.transpose(shared[0:E, 0, tt * P:tt * P + P], comb[:, tt], ident[:])
                last.then_inc(combT_ready, 1)

            def expert_in(f, k, side):
                if f.first == 0 and k == 0 and side == 0:
                    pe.wait_ge(experts_split, 2)
                claim(side, prod_done if side else silu_done, BLOCKS * f.n + k + 1)
                hi, lo = xn2T_hi[:, f.par], xn2T_lo[:, f.par]
                products(shared[:, side], [(wgu_hi[:, side, k], hi), (wgu_lo[:, side, k], hi), (wgu_hi[:, side, k], lo)]
                         ).then_inc(up_ready if side else gate_ready, 1)

            def expert_out(f, k):
                if k == 0:
                    if f.first == 0:
                        pe.wait_ge(down_loaded, 16)
                    wait(pe, ffnT_copied, f.n)
                    pe.wait_ge(prod_done, at(BLOCKS * f.n + 1))
                    hidden = f_prod[:, 0]
                else:
                    pe.wait_ge(act_done, at((BLOCKS - 1) * f.n + k))
                    hidden = f_act[:, k % 3]
                nc.tensor.matmul(down_bank[:], w_down[:, k], hidden, start=(k == 0),
                                 stop=(k == BLOCKS - 1)).then_inc(down_done, 1)

            def transpose_ffn(f):
                pe.wait_ge(ffnT_copied, at(f.n + 1))
                claim(1, result_ready, f.n + 1)
                for tt in range(TT):
                    cols = slice(tt * P, tt * P + P)
                    last = nc.tensor.transpose(shared[:, 1, cols], ffnT[:, cols], ident[:])
                last.then_inc(ffn_ready, 1)

            pe.wait_ge(consts_loaded, N_CONSTS)
            transpose_h(Batch(0))
            pe.wait_ge(w_split, 2)
            project_qk(Batch(0))
            project_v(Batch(0))
            for u in range(UNITS):
                max_unit(Batch(0), u)
            transpose_max(Batch(0))
            transpose_h(Batch(1))

            def iteration(t):
                b, n, p, f2 = t, t.plus(1), t.plus(-1), t.plus(-2)
                taken = 0
                for s in range(SLOTS):
                    units = []
                    for _ in range(MAX_SETS[s]):
                        units += range(4 * taken, 4 * taken + 4)
                        taken += 1
                    units = [u for u in units if n.exists]
                    work = [(t.plus(-back), k) for k, back in FFN_SLOTS[s] if t.plus(-back).exists]
                    for j in range(4):
                        if b.exists:
                            exp_unit(b, 4 * s + j)
                        for u in units[j * len(units) // 4:(j + 1) * len(units) // 4]:
                            max_unit(n, u)
                        if j // 2 < len(work):
                            f, k = work[j // 2]
                            expert_in(f, k, j % 2)
                    if s == 0 and p.exists:
                        value_set(p, SETS - 1)
                    if s > 0 and b.exists:
                        value_set(b, s - 1)
                    for f, k in work:
                        if k > 0:
                            expert_out(f, k - 1)
                    if s == 10 and f2.exists:
                        expert_out(f2, BLOCKS - 1)
                    if s == 11 and f2.exists:
                        transpose_ffn(f2)
                    if s == 0 and n.exists:
                        project_qk(n)
                    if s == 1 and n.exists:
                        project_v(n)
                    if s in (5, 9, 13) and b.exists:
                        transpose_o(b, (s - 5) // 4)
                    if p.exists:
                        if s == 1:
                            transpose_o(p, GROUPS - 1)
                        if s == 2:
                            transpose_o2(p)
                        if s == 3:
                            project_o(p)
                        if s == 5:
                            transpose_xn2(p)
                        if s == 6:
                            route(p)
                        if s == 8:
                            transpose_comb(p)
                    if s == 13 and n.exists:
                        transpose_max(n)
                    if s == 15 and t.plus(2).exists:
                        transpose_h(t.plus(2))

            def start_loop(t):
                left = [(hT_split, t.n + 2), (prod_done, BLOCKS * (t.n - 2) + 7)]
                assert last_reader == [(hT_split, t.first + 2), (prod_done, BLOCKS * (t.first - 2) + 7)]
                last_reader[:] = left

            def end_loop(t):
                assert [r[0] for r in last_reader] == [hT_split, prod_done]
                last_reader[:] = [(hT_split, t.n + 2), (prod_done, BLOCKS * (t.n - 2) + 7)]

            run_iterations(pe, iteration, start_loop, end_loop)

        @block.scalar
        def _(act):
            def split_hi(ready, value, bank, dst, done, bias=None):
                act.wait_ge(ready, at(value))
                if bias is None:
                    nc.scalar.activation(dst, shared[:, bank], ACT.Copy).then_inc(done, 1)
                else:
                    nc.scalar.activation(dst, shared[:, bank], ACT.Identity, bias=bias).then_inc(done, 1)

            def split_h(n):
                if n.first > 0:
                    act.wait_ge(v_ready, at(n.n))
                split_hi(hT_ready, n.n + 1, 0, hT_hi[:], hT_hi_ready)

            def split_qk(n):
                wait(act, qk_stored, 64 * n.n)
                for side in range(2):
                    split_hi(qk_ready, 2 * n.n + side + 1, 1 - side, qk_hi[:, side], qk_hi_ready,
                             bias=qk_bias[:, side:side + 1])

            def copy_max(n):
                wait(act, max_stored, 16 * n.n)
                act.wait_ge(maxT_ready, at(n.n + 1))
                nc.scalar.activation(maxT[:], shared[0:32, 0], ACT.Copy).then_inc(maxT_copied, 1)

            def exp_unit(b, u):
                act.wait_ge(scores_ready, at(UNITS * b.n + u + 1))
                if b.first == 0 and u == 0:
                    act.wait_ge(experts_split, 2)
                wait(act, pv_done, SETS * b.n + u // 4 - 1)
                nc.scalar.activation(probs[:, u % 8], exp_bank[:, u % 2], ACT.Exp,
                                     scale=float(DH) ** -0.5).then_inc(exp_done, 1)

            def copy_o(b, g):
                act.wait_ge(pv_done, at(SETS * b.n + TT * g + TT))
                wait(act, oq_ready, GROUPS * b.n + g - 1)
                nc.scalar.activation(oT[:, g % 2], out_bank[:], ACT.Copy).then_inc(oT_copied, 1)

            def exp_logits(b):
                act.wait_ge(logits_ready, at(b.n + 1))
                wait(act, route_step, ROUTE_STEPS * b.n)
                nc.scalar.activation(r_exp[:].rearrange("p t e -> p (t e)"), shared[:, 1, 0:TT * E], ACT.Exp,
                                     scale=-1.0).then_inc(logits_exp, 1)

            def copy_comb(b):
                act.wait_ge(combT_ready, at(b.n + 1))
                wait(act, comb_stored, 16 * b.n)
                nc.scalar.activation(combT[:], shared[0:E, 0], ACT.Copy).then_inc(combT_copied, 1)

            def gate_tanh(f, k):
                act.wait_ge(gate_ready, at(BLOCKS * f.n + k + 1))
                wait(act, silu_done, BLOCKS * f.n + k - 1)
                nc.scalar.activation(f_tanh[:, k % 2] if f.par == 0 else f_tanh[:, (k + 1) % 2], shared[:, 0],
                                     ACT.Tanh, scale=0.5).then_inc(tanh_done, 1)

            def copy_ffn(f):
                act.wait_ge(down_done, at(BLOCKS * (f.n + 1)))
                wait(act, ffn_ready, f.n)
                nc.scalar.activation(ffnT[:], down_bank[:], ACT.Copy).then_inc(ffnT_copied, 1)

            act.wait_ge(weights_loaded, 64)
            act.wait_ge(consts_loaded, N_CONSTS)
            nc.scalar.activation(w_hi[:], w_raw[:], ACT.Copy).then_inc(w_hi_ready, 1)
            nc.scalar.activation(gate_hi[:], gate_raw[:], ACT.Copy).then_inc(w_hi_ready, 1)
            split_h(Batch(0))
            split_qk(Batch(0))
            act.wait_ge(experts_loaded, 32)
            for side in range(2):
                nc.scalar.activation(wgu_hi[:, side].rearrange("p k m -> p (k m)"), raw_experts[side], ACT.Copy)\
                    .then_inc(experts_hi, 1)
            act.wait_ge(down_loaded, 16)
            nc.scalar.activation(w_down[:, 0], w_down[:, 0], ACT.Copy, scale=0.5).then_inc(down_loaded, 1)
            copy_max(Batch(0))

            def iteration(t):
                b, n, p, f2 = t, t.plus(1), t.plus(-1), t.plus(-2)
                for s in range(SLOTS):
                    if s == 0 and n.exists:
                        split_h(n)
                    if s == 1 and n.exists:
                        split_qk(n)
                    if s in (5, 9, 13) and b.exists:
                        copy_o(b, (s - 5) // 4)
                    if p.exists:
                        if s == 1:
                            copy_o(p, GROUPS - 1)
                        if s == 3:
                            split_hi(o2T_ready, p.n + 1, 0, o2T_hi[:], o2T_hi_ready)
                        if s == 6:
                            split_hi(xn2T_ready, p.n + 1, 0, xn2T_hi[:, p.par], xn2T_hi_ready)
                        if s == 7:
                            exp_logits(p)
                        if s == 9:
                            copy_comb(p)
                    if s == 11 and f2.exists:
                        copy_ffn(f2)
                    if s == 14 and n.exists:
                        copy_max(n)
                    work = [(t.plus(-back), k) for k, back in FFN_SLOTS[s] if t.plus(-back).exists]
                    for j in range(4):
                        if b.exists:
                            exp_unit(b, 4 * s + j)
                        if j in (1, 3) and j // 2 < len(work):
                            gate_tanh(*work[j // 2])

            run_iterations(act, iteration)

        @block.vector
        def _(dve):
            def settle(ins, done, value):
                ins.then_inc(done, 1)
                dve.wait_ge(done, at(value))

            def split_lo(hi_ready, value, bank, hi, lo, done, bias=None):
                dve.wait_ge(hi_ready, at(value))
                if bias is None:
                    ins = nc.vector.tensor_tensor(lo, shared[:, bank], hi.bitcast(F32), ALU.subtract)
                else:
                    ins = nc.vector.scalar_tensor_tensor(out=lo, in0=shared[:, bank], scalar=bias, in1=hi.bitcast(F32),
                                                         op0=ALU.add, op1=ALU.subtract)
                ins.then_inc(done, 1)

            def norm(which, n, src, dst, done):
                step = ln_step[which]
                for tt in range(TT):
                    nc.vector.bn_stats(stats[:, which, tt], src[:, tt])
                dve.drain()
                for tt in range(TT):
                    ins = nc.vector.bn_aggr(moments[:, which, tt], stats[:, which, tt])
                settle(ins, step, n.n + 1)
                nc.vector.tensor_scalar(var_eps[:, which], moments[:, which, :, 1], EPS, None, ALU.add)\
                    .then_inc(var_ready[which], 1)
                dve.wait_ge(rstd_ready[which], at(n.n + 1))
                for tt in range(TT):
                    ins = nc.vector.tensor_scalar(dst[:, tt], src[:, tt], moments[:, which, tt, 0:1],
                                                  rstd[:, which, tt:tt + 1], ALU.subtract, ALU.mult)
                ins.then_inc(done, 1)

            def norm_x(n):
                dve.wait_ge(x_loaded[n.par], at(16 * (n.pair + 1)))
                wait(dve, h_ready, n.n)
                norm(LN1, n, x_in[:, n.par], xn, xn_ready)

            def split_h(n):
                split_lo(hT_hi_ready, n.n + 1, 0, hT_hi[:], hT_lo[:], hT_split)

            def split_qk(n):
                wait(dve, qk_stored, 64 * n.n)
                for side in range(2):
                    split_lo(qk_hi_ready, 2 * n.n + side + 1, 1 - side, qk_hi[:, side], qk_lo[:, side], qk_lo_ready,
                             bias=qk_bias[:, side:side + 1])

            def copy_v(n):
                dve.wait_ge(v_ready, at(n.n + 1))
                if n.first >= 2:
                    dve.wait_ge(pv_done, at(SETS * (n.n - 1)))
                nc.vector.tensor_tensor(values[n.par][:, :, :, 0:DH],
                                        shared[:, 1].rearrange("p (t h d) -> p t h d", t=TT, h=H),
                                        bv_row[:].rearrange("p (h d) -> p h d", h=H).unsqueeze(1)
                                        .broadcast_to([P, TT, H, DH]), ALU.add)\
                    .then_inc(values_ready, 1)

            def take_max(n, u):
                g, qt, i = u // (4 * TT), (u // 4) % TT, u % 4
                if u == 0:
                    wait(dve, max_split, n.n)
                dve.wait_ge(max_scores, at(UNITS * n.n + u + 1))
                nc.vector.tensor_reduce(neg_max[:, qt, i, g:g + 1], max_bank[:, u % 2], AX_X, ALU.max,
                                        negate=True).then_inc(max_taken, 1)

            def split_max(n):
                dve.wait_ge(max_taken, at(UNITS * (n.n + 1)))
                wait(dve, maxT_ready, n.n)
                settle(nc.vector.tensor_copy(max_parts[:, :, :, 0].bitcast(F32R), neg_max[:]), max_hi, n.n + 1)
                nc.vector.tensor_tensor(max_parts[:, :, :, 1].bitcast(F32R), neg_max[:], max_parts[:, :, :, 0],
                                        ALU.subtract).then_inc(max_split, 1)

            def normalise_o(b, g):
                dve.wait_ge(oq_ready, at(GROUPS * b.n + g + 1))
                wait(dve, o_ready, GROUPS * b.n + g - 1)
                heads = shared[:, 1].rearrange("p (t i c) -> p t i c", t=TT, i=4)
                settle(nc.vector.reciprocal(o_rcp[:, g % 2], heads[:, :, :, DH]), o_rcp_ready, GROUPS * b.n + g + 1)
                if g == 0:
                    wait(dve, o2T_ready, b.n)
                nc.vector.tensor_tensor(o[:].rearrange("p t (i g d) -> p t i g d", i=4, g=GROUPS)[:, :, :, g],
                                        heads[:, :, :, 0:DH],
                                        o_rcp[:, g % 2].unsqueeze(3).broadcast_to([P, TT, 4, DH]), ALU.mult)\
                    .then_inc(o_ready, 1)

            def residual(b):
                dve.wait_ge(wo_ready, at(b.n + 1))
                wait(dve, xn2T_ready, b.n)
                dve.wait_ge(h_ready, at(b.n + 1))
                dve.wait_ge(x_beta_ready, at(b.n + 1))
                ins = nc.vector.tensor_tensor(y[:], shared[:, 1].rearrange("p (t d) -> p t d", t=TT),
                                              h_bo[:, b.par], ALU.add)
                ins
                settle(ins, y_ready, b.n + 1)
                norm(LN2, b, y, y, yn_ready)
                dve.wait_ge(yn_ready, at(b.n + 1))
                if b.first >= 2:
                    dve.wait_ge(result_stored, at(16 * (b.n - 1)))
                rows = gamma_row[:].unsqueeze(1).broadcast_to([P, TT, P])
                settle(nc.vector.tensor_tensor(y[:], y[:], rows, ALU.mult), x2_step, 2 * b.n + 1)
                settle(nc.vector.tensor_tensor(x2[:, b.par], y[:], x_beta[:, b.par], ALU.add), x2_step, 2 * b.n + 2)

            def norm_x2(b):
                norm(LN3, b, x2[:, b.par], y, xn2_ready)

            def route_groups(b):
                st = ROUTE_STEPS * b.n
                dve.wait_ge(logits_exp, at(b.n + 1))
                settle(nc.vector.tensor_scalar(r_den[:], r_exp[:], 1.0, None, ALU.add), route_step, st + 1)
                settle(nc.vector.reciprocal(r_sig[:], r_den[:]), route_step, st + 2)
                settle(nc.vector.tensor_tensor(r_sc[:], r_sig[:], route_bias[:].unsqueeze(1)
                                               .broadcast_to([P, TT, E]), ALU.add), route_step, st + 3)
                fours = r_sc[:].rearrange("p t (g a c) -> p (t g) a c", a=2, c=2)
                nc.vector.tensor_tensor(r_max[:], fours[:, :, :, 0], fours[:, :, :, 1], ALU.max).then_inc(route_step, 1)
                nc.vector.tensor_tensor(r_min[:], fours[:, :, :, 0], fours[:, :, :, 1], ALU.min).then_inc(route_step, 1)
                dve.wait_ge(route_step, at(st + 5))
                nc.vector.tensor_tensor(r_own[:], r_max[:], r_min[:], ALU.add).then_inc(route_step, 1)
                nc.vector.tensor_tensor(r_two[:, :, 0], r_max[:, :, 0], r_max[:, :, 1], ALU.add).then_inc(route_step, 1)
                dve.wait_ge(route_step, at(st + 7))
                settle(nc.vector.tensor_tensor(r_two[:, :, 1], r_own[:, :, 0], r_own[:, :, 1], ALU.max), route_step, st + 8)
                settle(nc.vector.tensor_tensor(r_grp[:].rearrange("p t g -> p (t g)"), r_two[:, :, 0], r_two[:, :, 1],
                                               ALU.max), route_step, st + 9)
                others = r_grp[:].unsqueeze(2).broadcast_to([P, TT, EG, EG])
                own = r_grp[:].unsqueeze(3).broadcast_to([P, TT, EG, EG])
                nc.vector.tensor_tensor(r_gt[:], others, own, ALU.is_gt).then_inc(route_step, 1)
                settle(nc.vector.tensor_tensor(r_eq[:], others, own, ALU.is_equal), route_step, st + 11)
                settle(nc.vector.tensor_tensor(r_eq[:], r_eq[:], ties[:].unsqueeze(1).broadcast_to([P, TT, EG, EG]),
                                               ALU.mult), route_step, st + 12)
                settle(nc.vector.tensor_tensor(r_gt[:], r_gt[:], r_eq[:], ALU.add), route_step, st + 13)
                settle(nc.vector.tensor_reduce(r_rank[:], r_gt[:], AX_X, ALU.add), route_step, st + 14)
                settle(nc.vector.tensor_scalar(r_open[:], r_rank[:], 4.0, None, ALU.is_lt), route_step, st + 15)

            def route_experts(b):
                group = lambda a: a[:].rearrange("p t (g e) -> p (t g) e", g=EG)
                nc.vector.tensor_tensor(group(r_masked), group(r_sc),
                                               r_open[:].rearrange("p t g -> p (t g)").unsqueeze(2)
                                               .broadcast_to([P, TT * EG, E // EG]), ALU.mult).then_inc(route_step, 1)
                dve.drain()
                for tt in range(TT):
                    nc.vector.max(r_top[:, tt], r_masked[:, tt])
                dve.drain()
                for tt in range(TT):
                    nc.vector.match_replace(r_rest[:, tt], r_top[:, tt], r_masked[:, tt], -3.0e38)
                dve.drain()
                settle(nc.vector.tensor_tensor(r_sel[:], r_rest[:], r_masked[:], ALU.not_equal), comb_step, 5 * b.n + 1)
                settle(nc.vector.tensor_tensor(r_w[:], r_sel[:], r_sig[:], ALU.mult), comb_step, 5 * b.n + 2)
                settle(nc.vector.tensor_reduce(r_sum[:, 0], r_w[:], AX_X, ALU.add), comb_step, 5 * b.n + 3)
                settle(nc.vector.tensor_scalar(r_sum[:, 1], r_sum[:, 0], 1e-20, None, ALU.add), comb_step, 5 * b.n + 4)
                settle(nc.vector.reciprocal(r_sum[:, 2], r_sum[:, 1]), comb_step, 5 * b.n + 5)
                wait(dve, combT_ready, b.n)
                nc.vector.scalar_tensor_tensor(out=comb[:], in0=r_w[:], scalar=ROUTE_SCALE / 2,
                                               in1=r_sum[:, 2].unsqueeze(2).broadcast_to([P, TT, E]),
                                               op0=ALU.mult, op1=ALU.mult).then_inc(comb_ready, 1)

            def silu(f, k):
                dve.wait_ge(tanh_done, at(BLOCKS * f.n + k + 1))
                slot = (k + f.par) % 2
                wait(dve, prod_done, BLOCKS * f.n + k - 1)
                nc.vector.scalar_tensor_tensor(out=f_silu[:, slot], in0=f_tanh[:, slot], scalar=1.0, in1=shared[:, 0],
                                               op0=ALU.add, op1=ALU.mult)\
                    .then_inc(silu_done, 1)

            def times_up(f, k):
                dve.wait_ge(up_ready, at(BLOCKS * f.n + k + 1))
                dve.wait_ge(silu_done, at(BLOCKS * f.n + k + 1))
                if k == 0:
                    wait(dve, down_done, BLOCKS * (f.n - 1) + 1)
                    dst = f_prod[:, 0]
                else:
                    wait(dve, act_done, (BLOCKS - 1) * f.n + k - 2)
                    dst = f_prod[:, 1 + k % 2]
                nc.vector.tensor_tensor(dst, f_silu[:, (k + f.par) % 2], shared[:, 1], ALU.mult)\
                    .then_inc(prod_done, 1)

            def finish(f):
                dve.wait_ge(ffn_ready, at(f.n + 1))
                nc.vector.tensor_tensor(x2[:, f.par], shared[:, 1].rearrange("p (t d) -> p t d", t=TT), x2[:, f.par],
                                        ALU.add).then_inc(result_ready, 1)

            norm_x(Batch(0))
            nc.vector.memset(out_bank[:], 0.0).then_inc(out_bank_set, 1)
            for i in range(2):
                nc.vector.memset(k_stack[i][:].bitcast(F32), 1.0).then_inc(ones_set, 1)
            dve.wait_ge(w_hi_ready, 2)
            nc.vector.tensor_tensor(w_lo[:], w_raw[:], w_hi[:].bitcast(F32), ALU.subtract).then_inc(w_split, 1)
            nc.vector.tensor_tensor(gate_lo[:], gate_raw[:], gate_hi[:].bitcast(F32), ALU.subtract).then_inc(w_split, 1)
            split_h(Batch(0))
            split_qk(Batch(0))
            dve.wait_ge(values_set, 2)
            copy_v(Batch(0))
            for u in range(UNITS):
                take_max(Batch(0), u)
                if u == 15:
                    norm_x(Batch(1))
            split_max(Batch(0))

            def iteration(t):
                n, p, f2 = t.plus(1), t.plus(-1), t.plus(-2)
                b = t
                taken = 0
                for s in range(SLOTS):
                    if s == 0 and n.exists:
                        split_h(n)
                    if s == 1 and n.exists:
                        split_qk(n)
                    if s == 2 and n.exists:
                        copy_v(n)
                    if s in (6, 10, 14) and b.exists:
                        normalise_o(b, (s - 6) // 4)
                    if p.exists:
                        if s == 2:
                            normalise_o(p, GROUPS - 1)
                        if s == 3:
                            split_lo(o2T_hi_ready, p.n + 1, 0, o2T_hi[:], o2T_lo[:], o2T_split)
                        if s == 4:
                            residual(p)
                        if s == 5:
                            norm_x2(p)
                        if s == 6:
                            split_lo(xn2T_hi_ready, p.n + 1, 0, xn2T_hi[:, p.par], xn2T_lo[:, p.par], xn2T_split)
                        if s == 7:
                            route_groups(p)
                        if s == 8:
                            route_experts(p)
                    if s == 12 and f2.exists:
                        finish(f2)
                    if s == 13 and n.exists:
                        split_max(n)
                    if s == 14 and t.plus(2).exists:
                        norm_x(t.plus(2))
                    units = []
                    for _ in range(MAX_SETS[s]):
                        units += range(4 * taken, 4 * taken + 4)
                        taken += 1
                    units = [u for u in units if n.exists]
                    work = [(t.plus(-back), k) for k, back in FFN_SLOTS[s] if t.plus(-back).exists]
                    for j in range(4):
                        for u in units[j * len(units) // 4:(j + 1) * len(units) // 4]:
                            take_max(n, u)
                        if j in (1, 3) and j // 2 < len(work):
                            silu(*work[j // 2])
                        if (j == 2 and work) or (j == 3 and len(work) == 2):
                            times_up(*work[j - 2])

            run_iterations(dve, iteration)

        @block.gpsimd
        def _(pool):
            def power(which, n):
                pool.wait_ge(var_ready[which], at(n.n + 1))
                wait(pool, (xn_ready, yn_ready, xn2_ready)[which], n.n)
                nc.gpsimd.tensor_tensor(rstd[:, which], var_eps[:, which], minus_half[:], ALU.pow)\
                    .then_inc(rstd_ready[which], 1)

            def add_positions(n):
                pool.wait_ge(xn_ready, at(n.n + 1))
                wait(pool, hT_ready, n.n)
                wait(pool, x_beta_ready, n.n)
                nc.gpsimd.tensor_tensor(h[:], xn[:], pos[:], ALU.add).then_inc(h_ready, 1)

            def add_biases(n):
                pool.wait_ge(h_ready, at(n.n + 1))
                if n.first >= 2:
                    pool.wait_ge(x2_step, at(2 * (n.n - 1)))
                row = lambda a: a[:].unsqueeze(1).broadcast_to([P, TT, P])
                nc.gpsimd.tensor_tensor(h_bo[:, n.par], h[:], row(bo_row), ALU.add).then_inc(h_bo_ready, 1)
                nc.gpsimd.tensor_tensor(x_beta[:, n.par], x_in[:, n.par], row(beta_row), ALU.add)\
                    .then_inc(x_beta_ready, 1)

            def weigh(f, k):
                if (k - 1) % 4 == 0:
                    pool.wait_ge(comb_loaded[(k - 1) // 4], at(32 * (f.n + 1)))
                pool.wait_ge(prod_done, at(BLOCKS * f.n + k + 1))
                if k <= 3:
                    wait(pool, down_done, BLOCKS * f.n)
                else:
                    pool.wait_ge(down_done, at(BLOCKS * f.n + k - 2))
                nc.gpsimd.tensor_tensor(f_act[:, k % 3], f_prod[:, 1 + k % 2], comb_all[:, (k - 1) % 8], ALU.mult)\
                    .then_inc(act_done, 1)

            nc.gpsimd.memset(minus_half[:], -0.5).then_inc(exponent_set, 1)
            pool.wait_ge(exponent_set, 1)
            power(LN1, Batch(0))
            for i in range(2):
                nc.gpsimd.memset(values[i][:, :, :, DH:DH + 1], 1.0).then_inc(values_set, 1)
            pool.wait_ge(consts_loaded, N_CONSTS)
            add_positions(Batch(0))
            add_biases(Batch(0))
            power(LN1, Batch(1))
            add_positions(Batch(1))
            pool.wait_ge(experts_hi, 2)
            for side in range(2):
                nc.gpsimd.tensor_tensor(wgu_lo[:, side].rearrange("p k m -> p (k m)"), raw_experts[side],
                                        wgu_hi[:, side].rearrange("p k m -> p (k m)").bitcast(F32), ALU.subtract)\
                    .then_inc(experts_split, 1)

            def iteration(t):
                n, p = t.plus(1), t.plus(-1)
                for s in range(SLOTS):
                    if s == 4 and p.exists:
                        power(LN2, p)
                    if s == 5 and p.exists:
                        power(LN3, p)
                    if s == 6 and n.exists:
                        add_biases(n)
                    if s == 14 and t.plus(2).exists:
                        power(LN1, t.plus(2))
                        add_positions(t.plus(2))
                    for k, back in FFN_SLOTS[s]:
                        f = t.plus(-back)
                        if f.exists and k > 0:
                            weigh(f, k)

            run_iterations(pool, iteration)


def positional_encoding():
    import numpy as np

    position = np.arange(T, dtype=np.float32)[:, None]
    rate = np.exp(np.arange(0, P, 2, dtype=np.float32) * np.float32(-np.log(10000.0) / P)).astype(np.float32)
    table = np.zeros((T, P), np.float32)
    table[:, 0::2] = np.sin(position * rate)
    table[:, 1::2] = np.cos(position * rate)
    return table


def kernel(**inputs):
    import numpy as np
    import concourse.bacc as bacc
    from concourse import mybir as mb
    from concourse.bass_utils import run_bass_kernel_spmd

    a = {k: np.asarray(v) for k, v in inputs.items()}
    attn = lambda k: a[f"L0_attn_{k}"]
    ffn = lambda k: a[f"L0_ffn_{k}"]
    gate_in = np.concatenate([ffn("sh_gate").T, ffn("w_gate").reshape(E * EI, P).T], axis=1)
    up_in = np.concatenate([ffn("sh_up").T, ffn("w_up").reshape(E * EI, P).T], axis=1)
    down = np.concatenate([ffn("sh_down").T, ffn("w_down").transpose(0, 2, 1).reshape(E * EI, P)], axis=0)
    arrays = {
        "x": attn("x"), "wq": attn("Wq"), "wk": attn("Wk"), "wv": attn("Wv"), "wo": attn("Wo"),
        "bq": attn("bq"), "bk": attn("bk"), "bv": attn("bv"), "bo": attn("bo"),
        "gamma": attn("gamma"), "beta": attn("beta"),
        "gate_wT": ffn("gate_w").T, "gate_bias": ffn("gate_bias"),
        "w_gateT": gate_in, "w_upT": up_in,
        "w_downT": down.reshape(BLOCKS, P, P).transpose(1, 0, 2),
        "pe_table": positional_encoding().reshape(TT, P, P).transpose(1, 0, 2),
        "identity": np.eye(P, dtype=np.float32),
        "tie_mask": np.broadcast_to(np.tril(np.ones((EG, EG), np.float32), -1), (P, EG, EG)),
    }
    nc = bacc.Bacc("TRN2", target_bir_lowering=False, num_devices=1)
    arrays = {f"in_{k}": np.ascontiguousarray(v) for k, v in arrays.items()}
    args = [nc.dram_tensor(k, v.shape, mb.dt.from_np(v.dtype), kind="ExternalInput").ap() for k, v in arrays.items()]
    out = nc.dram_tensor("out_y", (B, T, P), mb.dt.float32, kind="ExternalOutput").ap()
    build_layer(nc, *args, out)
    r = run_bass_kernel_spmd(nc, [arrays], core_ids=[0])
    return r.results[0]["out_y"]
```

```python
from contextlib import ExitStack

import concourse.bass as bass
from concourse import mybir

F32 = mybir.dt.float32
F32R = mybir.dt.float32r
ALU = mybir.AluOpType
ACT = mybir.ActivationFunctionType
AX_X = mybir.AxisListType.X

P = 128
B = 8
T = 512
TT = T // P
H = 16
DH = P // H
GROUPS = 4
E = 32
EG = 8
EI = 64
BLOCKS = 1 + E * EI // P
STACK = 3 * DH
UNITS = H * TT
SETS = UNITS // 4
SLOTS = 16
CHUNKS = 4
EPS = 1e-5
ROUTE_SCALE = 2.5
ROUTE_STEPS = 16
LN1, LN2, LN3 = range(3)

MAX_TILES = [0, 0, 7, 7, 2, 4, 6, 0, 0, 8, 8, 8, 7, 7, 0, 0]
MAX_FROM = [sum(MAX_TILES[:s]) for s in range(SLOTS)]
FFN_SLOTS = [[(7 + s, 2)] for s in range(10)] + [[(s, 1)] for s in range(5)] + [[(5, 1), (6, 1)]]


def max_tiles(s, j):
    return range(MAX_FROM[s] + j * MAX_TILES[s] // 4, MAX_FROM[s] + (j + 1) * MAX_TILES[s] // 4)


class Count:

    def __init__(self, trip, scale, base):
        self.trip, self.scale, self.base = trip, scale, base

    def __add__(self, k):
        return Count(self.trip, self.scale, self.base + k)

    def __sub__(self, k):
        return self + -k

    def __mul__(self, k):
        return Count(self.trip, self.scale * k, self.base * k)

    __rmul__ = __mul__


def at(count):
    return count.trip * count.scale + count.base if isinstance(count, Count) else count


class Batch:

    def __init__(self, first, trip=None):
        self.first, self.trip, self.par = first, trip, first % 2
        self.n = first if trip is None else Count(trip, 2, first)
        self.pair = first // 2 if trip is None else Count(trip, 1, first // 2)
        self.exists = 0 <= first < B

    def plus(self, k):
        return Batch(self.first + k, self.trip)


def wait(eng, sem, count):
    if isinstance(count, Count) or count > 0:
        eng.wait_ge(sem, at(count))


def build_layer(nc, x, wq, wk, wv, wo, bq, bk, bv, bo, gamma, beta, gate_wT, gate_bias, w_gateT,
                w_upT, w_downT, pe_table, identity, tie_mask, out):
    with ExitStack() as ctx:
        def sb(name, shape, dt=F32):
            return ctx.enter_context(nc.sbuf_tensor(name, shape, dt))

        def ps(name, shape):
            return ctx.enter_context(nc.psum_tensor(name, shape, F32))

        def sem(name):
            return ctx.enter_context(nc.semaphore(name))

        ident = sb("ident", [P, P])
        ties = sb("ties", [P, EG, EG])
        pos = sb("pos", [P, TT, P])
        w_hi = sb("w_hi", [P, 4, P], F32R)
        w_lo = sb("w_lo", [P, 4, P], F32R)
        gate_raw = sb("gate_raw", [P, E])
        gate_hi = sb("gate_hi", [P, E], F32R)
        gate_lo = sb("gate_lo", [P, E], F32R)
        wgu_hi = sb("wgu_hi", [P, 2, BLOCKS, P], F32R)
        wgu_lo = sb("wgu_lo", [P, 2, BLOCKS, P], F32R)
        w_down = sb("w_down", [P, BLOCKS, P])
        qk_bias = sb("qk_bias", [P, 2])
        bv_row = sb("bv_row", [P, P])
        bo_row = sb("bo_row", [P, P])
        gamma_row = sb("gamma_row", [P, P])
        beta_row = sb("beta_row", [P, P])
        route_bias = sb("route_bias", [P, E])
        minus_half = sb("minus_half", [P, TT])

        x_in = sb("x_in", [P, 2, TT, P])
        x_beta = sb("x_beta", [P, 2, TT, P])
        xn = sb("xn", [P, TT, P])
        h = sb("h", [P, TT, P])
        h_bo = sb("h_bo", [P, 2, TT, P])
        hT_hi = sb("hT_hi", [P, T], F32R)
        hT_lo = sb("hT_lo", [P, T], F32R)
        qk_parts = sb("qk_parts", [P, 2, 2, T], F32R)
        q_stack = [sb(f"q_stack{i}", [P, GROUPS, T], F32R) for i in range(2)]
        k_stack = [sb(f"k_stack{i}", [P, GROUPS, T], F32R) for i in range(2)]
        values = [sb(f"values{i}", [P, TT, H, DH + 1]) for i in range(2)]
        neg_max = sb("neg_max", [P, TT, 4, GROUPS])
        max_parts = sb("max_parts", [P, TT, 4, 2, GROUPS])
        maxT = sb("maxT", [4 * 2 * GROUPS, T])
        probs = sb("probs", [P, 8, T])
        oT = sb("oT", [P, 2, T])
        o_rcp = sb("o_rcp", [P, 2, TT, 4])
        o = sb("o", [P, TT, P])
        o2T_hi = sb("o2T_hi", [P, T], F32R)
        o2T_lo = sb("o2T_lo", [P, T], F32R)
        y = sb("y", [P, TT, P])
        x2 = sb("x2", [P, 2, TT, P])
        xn2T_hi = sb("xn2T_hi", [P, 2, T], F32R)
        xn2T_lo = sb("xn2T_lo", [P, 2, T], F32R)
        stats = sb("stats", [P, 3, TT, 6])
        moments = sb("moments", [P, 3, TT, 2])
        var_eps = sb("var_eps", [P, 3, TT])
        rstd = sb("rstd", [P, 3, TT])
        r_exp = sb("r_exp", [P, TT, E])
        r_den = sb("r_den", [P, TT, E])
        r_sig = sb("r_sig", [P, TT, E])
        r_sc = sb("r_sc", [P, TT, E])
        r_max = sb("r_max", [P, TT * EG, 2])
        r_min = sb("r_min", [P, TT * EG, 2])
        r_own = sb("r_own", [P, TT * EG, 2])
        r_two = sb("r_two", [P, TT * EG, 2])
        r_grp = sb("r_grp", [P, TT, EG])
        r_gt = sb("r_gt", [P, TT, EG, EG])
        r_eq = sb("r_eq", [P, TT, EG, EG])
        r_rank = sb("r_rank", [P, TT, EG])
        r_open = sb("r_open", [P, TT, EG])
        r_masked = sb("r_masked", [P, TT, E])
        r_top = sb("r_top", [P, TT, 8])
        r_rest = sb("r_rest", [P, TT, E])
        r_sel = sb("r_sel", [P, TT, E])
        r_w = sb("r_w", [P, TT, E])
        r_sum = sb("r_sum", [P, 3, TT])
        comb = sb("comb", [P, TT, E])
        combT = sb("combT", [E, T])
        comb_all = sb("comb_all", [P, 8, T])
        f_tanh = sb("f_tanh", [P, 2, T])
        f_silu = sb("f_silu", [P, 2, T])
        f_up = sb("f_up", [P, 2, T])
        f_act = sb("f_act", [P, 4, T])
        ffnT = sb("ffnT", [P, T])

        max_bank = ps("max_bank", [P, 2, T])
        exp_bank = ps("exp_bank", [P, 2, T])
        out_bank = ps("out_bank", [P, T])
        down_bank = ps("down_bank", [P, T])
        shared = ps("shared", [P, 2, T])

        w_raw = y
        raw_experts = [comb_all[:].rearrange("p a b -> p (a b)")[:, 0:BLOCKS * P],
                       probs[:].rearrange("p a b -> p (a b)")[:, 0:BLOCKS * P]]

        qk_scratch = nc.dram_tensor("qk_scratch", (2, 2, P, 3, T), F32).ap()
        max_scratch = nc.dram_tensor("max_scratch", (2, 4 * 2 * GROUPS, T), F32).ap()
        comb_scratch = nc.dram_tensor("comb_scratch", (2, E, T), F32).ap()

        consts_loaded = sem("consts_loaded")
        weights_loaded = sem("weights_loaded")
        experts_loaded = sem("experts_loaded")
        down_loaded = sem("down_loaded")
        ones_set = sem("ones_set")
        values_set = sem("values_set")
        out_bank_set = sem("out_bank_set")
        h_bo_ready = sem("h_bo_ready")
        comb_step = sem("comb_step")
        exponent_set = sem("exponent_set")
        w_hi_ready = sem("w_hi_ready")
        w_split = sem("w_split")
        experts_hi = sem("experts_hi")
        experts_split = sem("experts_split")
        x_loaded = [sem(f"x_loaded{i}") for i in range(2)]
        ln_step = [sem(f"ln_step{i}") for i in range(3)]
        var_ready = [sem(f"var_ready{i}") for i in range(3)]
        rstd_ready = [sem(f"rstd_ready{i}") for i in range(3)]
        xn_ready = sem("xn_ready")
        h_ready = sem("h_ready")
        x_beta_ready = sem("x_beta_ready")
        hT_ready = sem("hT_ready")
        hT_hi_ready = sem("hT_hi_ready")
        hT_split = sem("hT_split")
        qk_ready = sem("qk_ready")
        qk_hi_ready = sem("qk_hi_ready")
        qk_lo_ready = sem("qk_lo_ready")
        qk_stored = sem("qk_stored")
        stack_loaded = sem("stack_loaded")
        v_ready = sem("v_ready")
        values_ready = sem("values_ready")
        max_scores = sem("max_scores")
        max_taken = sem("max_taken")
        max_hi = sem("max_hi")
        max_split = sem("max_split")
        maxT_ready = sem("maxT_ready")
        maxT_copied = sem("maxT_copied")
        max_stored = sem("max_stored")
        max_loaded = sem("max_loaded")
        scores_ready = sem("scores_ready")
        exp_done = sem("exp_done")
        pv_done = sem("pv_done")
        oT_copied = sem("oT_copied")
        oq_ready = sem("oq_ready")
        o_rcp_ready = sem("o_rcp_ready")
        o_ready = sem("o_ready")
        o2T_ready = sem("o2T_ready")
        o2T_hi_ready = sem("o2T_hi_ready")
        o2T_split = sem("o2T_split")
        wo_ready = sem("wo_ready")
        y_ready = sem("y_ready")
        yn_ready = sem("yn_ready")
        x2_step = sem("x2_step")
        xn2_ready = sem("xn2_ready")
        xn2T_ready = sem("xn2T_ready")
        xn2T_hi_ready = sem("xn2T_hi_ready")
        xn2T_split = sem("xn2T_split")
        logits_ready = sem("logits_ready")
        logits_exp = sem("logits_exp")
        route_step = sem("route_step")
        comb_ready = sem("comb_ready")
        combT_ready = sem("combT_ready")
        combT_copied = sem("combT_copied")
        comb_stored = sem("comb_stored")
        comb_loaded = [sem(f"comb_loaded{i}") for i in range(CHUNKS)]
        gate_ready = sem("gate_ready")
        up_ready = sem("up_ready")
        tanh_done = sem("tanh_done")
        silu_done = sem("silu_done")
        up_copied = sem("up_copied")
        weighed = sem("weighed")
        act_done = sem("act_done")
        down_done = sem("down_done")
        ffnT_copied = sem("ffnT_copied")
        ffn_ready = sem("ffn_ready")
        result_ready = sem("result_ready")
        result_stored = sem("result_stored")

        x_view = x.rearrange("b (t p) d -> b p t d", p=P)
        out_view = out.rearrange("b (t p) d -> b p t d", p=P)
        N_CONSTS = 16 * 11
        LOOP_FROM, LOOP_TRIPS = 2, 2

        def run_iterations(eng, iteration, start_loop=None, end_loop=None):
            for t in range(LOOP_FROM):
                iteration(Batch(t))
            with eng.Fori(0, LOOP_TRIPS) as trip:
                eng.get_value_cache().nocache = True
                if start_loop:
                    start_loop(Batch(LOOP_FROM, trip))
                for u in range(2):
                    iteration(Batch(LOOP_FROM + u, trip))
            if end_loop:
                end_loop(Batch(LOOP_FROM + 2 * LOOP_TRIPS))
            for t in range(LOOP_FROM + 2 * LOOP_TRIPS, B + 2):
                iteration(Batch(t))

        block = ctx.enter_context(nc.Block())

        @block.sync
        def _(sp):
            def stack_qk(n):
                scratch = qk_scratch[n.par]
                sp.wait_ge(qk_hi_ready, at(2 * n.n + 2))
                sp.dma_start(scratch[:, :, 0].rearrange("s p n -> p s n"), qk_parts[:, :, 0].bitcast(F32))\
                    .then_inc(qk_stored, 16)
                sp.dma_start(scratch[1, :, 2], qk_parts[:, 1, 0].bitcast(F32)).then_inc(qk_stored, 16)
                sp.wait_ge(qk_lo_ready, at(2 * n.n + 1))
                sp.dma_start(scratch[0, :, 1:3], qk_parts[:, 0].bitcast(F32)).then_inc(qk_stored, 16)
                sp.wait_ge(qk_lo_ready, at(2 * n.n + 2))
                sp.dma_start(scratch[1, :, 1], qk_parts[:, 1, 1].bitcast(F32)).then_inc(qk_stored, 16)
                wait(sp, scores_ready, UNITS * (n.n - 1))
                sp.wait_ge(qk_stored, at(64 * n.n + 64))
                for side, stack in enumerate((q_stack, k_stack)):
                    rows = scratch[side].rearrange("(i g d) j n -> i (d j) g n", g=GROUPS, d=DH)
                    for i in range(4):
                        row = 32 * i
                        sp.dma_start(stack[n.par][row:row + STACK].bitcast(F32), rows[i]).then_inc(stack_loaded, 16)

            def stack_max(n):
                sp.wait_ge(maxT_copied, at(n.n + 1))
                sp.dma_start(max_scratch[n.par], maxT[:]).then_inc(max_stored, 16)
                sp.wait_ge(max_stored, at(16 * n.n + 16))
                rows = max_scratch[n.par].rearrange("(i a g) n -> i a g n", a=2, g=GROUPS)
                for i in range(4):
                    row = 32 * i + STACK
                    sp.dma_start(q_stack[n.par][row:row + 2].bitcast(F32), rows[i]).then_inc(max_loaded, 16)

            def store_comb(f):
                sp.wait_ge(combT_copied, at(f.n + 1))
                sp.dma_start(comb_scratch[f.par], combT[:]).then_inc(comb_stored, 16)
                sp.wait_ge(comb_stored, at(16 * f.n + 16))

            def broadcast_comb(f, c):
                rows = comb_scratch[f.par].rearrange("(k a) n -> a k n", a=2)
                wait(sp, weighed, (BLOCKS - 1) * f.n + 4 * (c - 2) + 4)
                slot = 4 * (c % 2)
                for a in range(2):
                    src = rows[a, 4 * c:4 * c + 4].unsqueeze(0).broadcast_to([EI, 4, T])
                    sp.dma_start(comb_all[EI * a:EI * a + EI, slot:slot + 4], src).then_inc(comb_loaded[c], 16)

            def store_result(f):
                sp.wait_ge(result_ready, at(f.n + 1))
                sp.dma_start(out_view[at(f.n)], x2[:, f.par]).then_inc(result_stored, 16)

            for n in (Batch(0), Batch(1)):
                sp.dma_start(x_in[:, n.par], x_view[n.n]).then_inc(x_loaded[n.par], 16)
            for dst, src in ((ident[:], identity), (pos[:], pe_table), (ties[:], tie_mask),
                             (bv_row[:], bv.partition_broadcast(P)), (bo_row[:], bo.partition_broadcast(P)),
                             (gamma_row[:], gamma.partition_broadcast(P)),
                             (beta_row[:], beta.partition_broadcast(P)),
                             (route_bias[:], gate_bias.partition_broadcast(P)),
                             (gate_raw[:], gate_wT), (qk_bias[:, 0:1], bq.unsqueeze(1)),
                             (qk_bias[:, 1:2], bk.unsqueeze(1))):
                sp.dma_start(dst, src).then_inc(consts_loaded, 16)
            for n, w in enumerate((wq, wk, wv, wo)):
                sp.dma_start(w_raw[:, n], w).then_inc(weights_loaded, 16)
            for side, w in enumerate((w_gateT, w_upT)):
                sp.dma_start(raw_experts[side], w).then_inc(experts_loaded, 16)
            sp.dma_start(w_down[:], w_downT).then_inc(down_loaded, 16)
            sp.wait_ge(ones_set, 2)
            stack_qk(Batch(0))
            stack_max(Batch(0))
            stack_qk(Batch(1))

            def iteration(t):
                if t.plus(-2).exists:
                    broadcast_comb(t.plus(-2), 3)
                if t.plus(-1).exists:
                    if t.first == 1:
                        sp.wait_ge(experts_split, 2)
                    store_comb(t.plus(-1))
                    broadcast_comb(t.plus(-1), 0)
                    broadcast_comb(t.plus(-1), 1)
                if t.plus(-2).exists:
                    store_result(t.plus(-2))
                if t.plus(1).exists:
                    stack_max(t.plus(1))
                if t.plus(-1).exists:
                    broadcast_comb(t.plus(-1), 2)
                if t.plus(2).exists:
                    stack_qk(t.plus(2))

            run_iterations(sp, iteration)
            sp.wait_ge(result_stored, 16 * B)

        @block.tensor
        def _(pe):
            last_reader = [None, None]

            def claim(bank, done, value):
                if last_reader[bank]:
                    done_before, value_before = last_reader[bank]
                    pe.wait_ge(done_before, at(value_before))
                last_reader[bank] = (done, value)

            def products(dst, pairs, start=True, stop=True):
                for n, (left, right) in enumerate(pairs):
                    last = nc.tensor.matmul(dst, left, right, start=start and n == 0,
                                            stop=stop and n == len(pairs) - 1)
                return last

            def transpose_h(n):
                pe.wait_ge(h_ready, at(n.n + 1))
                claim(1, hT_split, n.n + 1)
                for tt in range(TT):
                    last = nc.tensor.transpose(shared[:, 1, tt * P:tt * P + P], h[:, tt], ident[:])
                last.then_inc(hT_ready, 1)

            def project_qk(n):
                pe.wait_ge(hT_split, at(n.n + 1))
                for side in range(2):
                    claim(side, qk_lo_ready, 2 * n.n + side + 1)
                    products(shared[:, side], [(w_hi[:, side], hT_hi[:]), (w_lo[:, side], hT_hi[:]),
                                               (w_hi[:, side], hT_lo[:])]).then_inc(qk_ready, 1)

            def project_v(n):
                claim(1, values_ready, n.n + 1)
                for tt in range(TT):
                    cols = slice(tt * P, tt * P + P)
                    last = products(shared[:, 1, cols], [(hT_hi[:, cols], w_hi[:, 2]), (hT_hi[:, cols], w_lo[:, 2]),
                                                         (hT_lo[:, cols], w_hi[:, 2])])
                last.then_inc(v_ready, 1)

            def max_unit(n, u):
                g, qt, i = u // (4 * TT), (u // 4) % TT, u % 4
                if u == 0:
                    pe.wait_ge(stack_loaded, at(16 * 8 * (n.n + 1)))
                wait(pe, max_taken, UNITS * n.n + u - 1)
                rows = slice(32 * i, 32 * i + STACK)
                nc.tensor.matmul(max_bank[:, u % 2], q_stack[n.par][rows, g, qt * P:qt * P + P],
                                 k_stack[n.par][rows, g, :], start=True, stop=True).then_inc(max_scores, 1)

            def transpose_max(n):
                pe.wait_ge(max_split, at(n.n + 1))
                claim(0, maxT_copied, n.n + 1)
                for tt in range(TT):
                    last = nc.tensor.transpose(shared[0:32, 0, tt * P:tt * P + P],
                                               max_parts[:, tt].rearrange("p i a g -> p (i a g)"), ident[:])
                last.then_inc(maxT_ready, 1)

            def exp_unit(b, u):
                g, kt, i = u // (4 * TT), (u // 4) % TT, u % 4
                if u == 0:
                    pe.wait_ge(max_loaded, at(64 * (b.n + 1)))
                wait(pe, exp_done, UNITS * b.n + u - 1)
                rows = slice(32 * i, 32 * i + STACK + 2)
                nc.tensor.matmul(exp_bank[:, u % 2], k_stack[b.par][rows, g, kt * P:kt * P + P],
                                 q_stack[b.par][rows, g, :], start=True, stop=True).then_inc(scores_ready, 1)

            def value_set(b, s):
                g, kt = s // TT, s % TT
                if s == 0:
                    pe.wait_ge(values_ready, at(b.n + 1))
                if s == 0 and b.first == 0:
                    pe.wait_ge(out_bank_set, 1)
                if kt == 0:
                    wait(pe, oT_copied, GROUPS * b.n + g)
                pe.wait_ge(exp_done, at(UNITS * b.n + 4 * s + 4))
                for i in range(4):
                    last = nc.tensor.matmul(out_bank[32 * i:32 * i + DH + 1], values[b.par][:, kt, 4 * i + g, :],
                                            probs[:, (4 * s + i) % 8], start=(kt == 0), stop=(kt == TT - 1))
                last.then_inc(pv_done, 1)

            def transpose_o(b, g):
                pe.wait_ge(oT_copied, at(GROUPS * b.n + g + 1))
                claim(0, o_ready, GROUPS * b.n + g + 1)
                for tt in range(TT):
                    cols = slice(tt * P, tt * P + P)
                    last = nc.tensor.transpose(shared[:, 0, cols], oT[:, g % 2, cols], ident[:])
                last.then_inc(oq_ready, 1)

            def transpose_o2(b):
                pe.wait_ge(o_ready, at(GROUPS * (b.n + 1)))
                claim(1, o2T_split, b.n + 1)
                for tt in range(TT):
                    last = nc.tensor.transpose(shared[:, 1, tt * P:tt * P + P], o[:, tt], ident[:])
                last.then_inc(o2T_ready, 1)

            def project_o(b):
                pe.wait_ge(o2T_split, at(b.n + 1))
                claim(1, y_ready, b.n + 1)
                for tt in range(TT):
                    cols = slice(tt * P, tt * P + P)
                    last = products(shared[:, 1, cols], [(o2T_hi[:, cols], w_hi[:, 3]), (o2T_hi[:, cols], w_lo[:, 3]),
                                                         (o2T_lo[:, cols], w_hi[:, 3])])
                last.then_inc(wo_ready, 1)

            def transpose_xn2(b):
                pe.wait_ge(xn2_ready, at(b.n + 1))
                claim(1, xn2T_split, b.n + 1)
                for tt in range(TT):
                    last = nc.tensor.transpose(shared[:, 1, tt * P:tt * P + P], y[:, tt], ident[:])
                last.then_inc(xn2T_ready, 1)

            def route(b):
                pe.wait_ge(xn2T_split, at(b.n + 1))
                claim(1, logits_exp, b.n + 1)
                hi, lo = xn2T_hi[:, b.par], xn2T_lo[:, b.par]
                for tt in range(TT):
                    cols = slice(tt * P, tt * P + P)
                    last = products(shared[:, 1, tt * E:tt * E + E], [(hi[:, cols], gate_hi[:]), (hi[:, cols], gate_lo[:]),
                                                                      (lo[:, cols], gate_hi[:])])
                last.then_inc(logits_ready, 1)

            def transpose_comb(b):
                pe.wait_ge(comb_ready, at(b.n + 1))
                claim(1, combT_copied, b.n + 1)
                for tt in range(TT):
                    last = nc.tensor.transpose(shared[0:E, 1, tt * P:tt * P + P], comb[:, tt], ident[:])
                last.then_inc(combT_ready, 1)

            def expert_in(f, k, side):
                if f.first == 0 and k == 0 and side == 0:
                    pe.wait_ge(experts_split, 2)
                claim(side, up_copied if side else silu_done, BLOCKS * f.n + k + 1)
                hi, lo = xn2T_hi[:, f.par], xn2T_lo[:, f.par]
                products(shared[:, side], [(wgu_hi[:, side, k], hi), (wgu_lo[:, side, k], hi), (wgu_hi[:, side, k], lo)]
                         ).then_inc(up_ready if side else gate_ready, 1)

            def expert_out(f, k):
                if k == 0:
                    if f.first == 0:
                        pe.wait_ge(down_loaded, 16)
                    wait(pe, ffnT_copied, f.n)
                pe.wait_ge(act_done, at(BLOCKS * f.n + k + 1))
                hidden = f_act[:, 1 + k % 3 if k else 0]
                nc.tensor.matmul(down_bank[:], w_down[:, k], hidden, start=(k == 0),
                                 stop=(k == BLOCKS - 1)).then_inc(down_done, 1)

            def transpose_ffn(f):
                pe.wait_ge(ffnT_copied, at(f.n + 1))
                claim(1, result_ready, f.n + 1)
                for tt in range(TT):
                    cols = slice(tt * P, tt * P + P)
                    last = nc.tensor.transpose(shared[:, 1, cols], ffnT[:, cols], ident[:])
                last.then_inc(ffn_ready, 1)

            pe.wait_ge(consts_loaded, N_CONSTS)
            transpose_h(Batch(0))
            pe.wait_ge(w_split, 2)
            project_qk(Batch(0))
            project_v(Batch(0))
            for u in range(UNITS):
                max_unit(Batch(0), u)
            transpose_max(Batch(0))
            transpose_h(Batch(1))
            project_qk(Batch(1))

            def iteration(t):
                b, n, p, f2 = t, t.plus(1), t.plus(-1), t.plus(-2)
                for s in range(SLOTS):
                    work = [(t.plus(-back), k) for k, back in FFN_SLOTS[s] if t.plus(-back).exists]
                    for j in range(4):
                        if b.exists:
                            exp_unit(b, 4 * s + j)
                        for u in max_tiles(s, j) if n.exists else ():
                            max_unit(n, u)
                        if len(work) == 2:
                            expert_in(*work[j // 2], j % 2)
                        elif work and j in (0, 2):
                            expert_in(*work[0], j // 2)
                        if j == 1 and s == 0 and p.exists:
                            value_set(p, SETS - 1)
                        if j == 1 and s > 0 and b.exists:
                            value_set(b, s - 1)
                        if (s, j) == (14, 2) and n.exists:
                            transpose_max(n)
                        if j in (1, 3):
                            for f, k in work[j // 2:j // 2 + 1] if len(work) == 2 else work[:j // 2]:
                                if k > 0:
                                    expert_out(f, k - 1)
                    if s == 10 and f2.exists:
                        expert_out(f2, BLOCKS - 1)
                    if s == 11 and f2.exists:
                        transpose_ffn(f2)
                    if s == 0 and n.exists:
                        project_v(n)
                    if s in (5, 9, 13) and b.exists:
                        transpose_o(b, (s - 5) // 4)
                    if p.exists:
                        if s == 1:
                            transpose_o(p, GROUPS - 1)
                        if s == 2:
                            transpose_o2(p)
                        if s == 3:
                            project_o(p)
                        if s == 5:
                            transpose_xn2(p)
                        if s == 6:
                            route(p)
                        if s == 8:
                            transpose_comb(p)
                    if s == 12 and t.plus(2).exists:
                        transpose_h(t.plus(2))
                    if s == 14 and t.plus(2).exists:
                        project_qk(t.plus(2))

            def start_loop(t):
                blocks_done = BLOCKS * (t.n - 2) + 7
                assert last_reader == [(silu_done, BLOCKS * (t.first - 2) + 7), (up_copied, BLOCKS * (t.first - 2) + 7)]
                last_reader[:] = [(silu_done, blocks_done), (up_copied, blocks_done)]

            def end_loop(t):
                assert [done for done, _ in last_reader] == [silu_done, up_copied]
                last_reader[:] = [(done, BLOCKS * (t.n - 2) + 7) for done in (silu_done, up_copied)]

            run_iterations(pe, iteration, start_loop, end_loop)

        @block.scalar
        def _(act):
            def split_hi(ready, value, bank, dst, done, bias=None):
                act.wait_ge(ready, at(value))
                if bias is None:
                    nc.scalar.activation(dst, shared[:, bank], ACT.Copy).then_inc(done, 1)
                else:
                    nc.scalar.activation(dst, shared[:, bank], ACT.Identity, bias=bias).then_inc(done, 1)

            def split_h(n):
                if n.first > 0:
                    act.wait_ge(v_ready, at(n.n))
                split_hi(hT_ready, n.n + 1, 1, hT_hi[:], hT_hi_ready)

            def split_qk(n):
                wait(act, qk_stored, 64 * n.n)
                for side in range(2):
                    split_hi(qk_ready, 2 * n.n + side + 1, side, qk_parts[:, side, 0], qk_hi_ready,
                             bias=qk_bias[:, side:side + 1])

            def copy_max(n):
                wait(act, max_stored, 16 * n.n)
                act.wait_ge(maxT_ready, at(n.n + 1))
                nc.scalar.activation(maxT[:], shared[0:32, 0], ACT.Copy).then_inc(maxT_copied, 1)

            def load_x(n):
                act.wait_ge(xn_ready, at(n.n - 1))
                act.wait_ge(x_beta_ready, at(n.n - 1))
                act.dma_start(x_in[:, n.par], x_view[at(n.n)]).then_inc(x_loaded[n.par], 16)

            def exp_unit(b, u):
                act.wait_ge(scores_ready, at(UNITS * b.n + u + 1))
                if b.first == 0 and u == 0:
                    act.wait_ge(experts_split, 2)
                wait(act, pv_done, SETS * b.n + u // 4 - 1)
                nc.scalar.activation(probs[:, u % 8], exp_bank[:, u % 2], ACT.Exp,
                                     scale=float(DH) ** -0.5).then_inc(exp_done, 1)

            def copy_o(b, g):
                act.wait_ge(pv_done, at(SETS * b.n + TT * g + TT))
                wait(act, oq_ready, GROUPS * b.n + g - 1)
                nc.scalar.activation(oT[:, g % 2], out_bank[:], ACT.Copy).then_inc(oT_copied, 1)

            def exp_logits(b):
                act.wait_ge(logits_ready, at(b.n + 1))
                wait(act, route_step, ROUTE_STEPS * b.n)
                nc.scalar.activation(r_exp[:].rearrange("p t e -> p (t e)"), shared[:, 1, 0:TT * E], ACT.Exp,
                                     scale=-1.0).then_inc(logits_exp, 1)

            def copy_comb(b):
                act.wait_ge(combT_ready, at(b.n + 1))
                wait(act, comb_stored, 16 * b.n)
                nc.scalar.activation(combT[:], shared[0:E, 1], ACT.Copy).then_inc(combT_copied, 1)

            def gate_tanh(f, k):
                act.wait_ge(gate_ready, at(BLOCKS * f.n + k + 1))
                wait(act, silu_done, BLOCKS * f.n + k - 1)
                nc.scalar.activation(f_tanh[:, (k + f.par) % 2], shared[:, 0],
                                     ACT.Tanh, scale=0.5).then_inc(tanh_done, 1)

            def copy_up(f, k):
                act.wait_ge(up_ready, at(BLOCKS * f.n + k + 1))
                wait(act, act_done, BLOCKS * f.n + k - 1)
                nc.scalar.activation(f_up[:, (k + f.par) % 2], shared[:, 1], ACT.Copy).then_inc(up_copied, 1)

            def copy_ffn(f):
                act.wait_ge(down_done, at(BLOCKS * (f.n + 1)))
                wait(act, ffn_ready, f.n)
                nc.scalar.activation(ffnT[:], down_bank[:], ACT.Copy).then_inc(ffnT_copied, 1)

            act.wait_ge(weights_loaded, 64)
            act.wait_ge(consts_loaded, N_CONSTS)
            nc.scalar.activation(w_hi[:], w_raw[:], ACT.Copy).then_inc(w_hi_ready, 1)
            nc.scalar.activation(gate_hi[:], gate_raw[:], ACT.Copy).then_inc(w_hi_ready, 1)
            split_h(Batch(0))
            split_qk(Batch(0))
            act.wait_ge(experts_loaded, 32)
            for side in range(2):
                nc.scalar.activation(wgu_hi[:, side].rearrange("p k m -> p (k m)"), raw_experts[side], ACT.Copy)\
                    .then_inc(experts_hi, 1)
            act.wait_ge(down_loaded, 16)
            nc.scalar.activation(w_down[:, 0], w_down[:, 0], ACT.Copy, scale=0.5).then_inc(down_loaded, 1)
            copy_max(Batch(0))
            split_h(Batch(1))
            split_qk(Batch(1))

            def iteration(t):
                b, n, p, f2 = t, t.plus(1), t.plus(-1), t.plus(-2)
                for s in range(SLOTS):
                    if s == 0 and t.plus(2).exists:
                        load_x(t.plus(2))
                    if s == 13 and t.plus(2).exists:
                        split_h(t.plus(2))
                    if s == 15 and t.plus(2).exists:
                        split_qk(t.plus(2))
                    if s in (5, 9, 13) and b.exists:
                        copy_o(b, (s - 5) // 4)
                    if p.exists:
                        if s == 1:
                            copy_o(p, GROUPS - 1)
                        if s == 3:
                            split_hi(o2T_ready, p.n + 1, 1, o2T_hi[:], o2T_hi_ready)
                        if s == 6:
                            split_hi(xn2T_ready, p.n + 1, 1, xn2T_hi[:, p.par], xn2T_hi_ready)
                        if s == 7:
                            exp_logits(p)
                        if s == 9:
                            copy_comb(p)
                    if s == 11 and f2.exists:
                        copy_ffn(f2)
                    work = [(t.plus(-back), k) for k, back in FFN_SLOTS[s] if t.plus(-back).exists]
                    for j in range(4):
                        if b.exists:
                            exp_unit(b, 4 * s + j)
                        if j in (0, 2) and j // 2 < len(work):
                            gate_tanh(*work[j // 2])
                        if j in (1, 3) and len(work) == 2:
                            copy_up(*work[j // 2])
                        if j == 2 and len(work) == 1:
                            copy_up(*work[0])
                        if (s, j) == (14, 3) and n.exists:
                            copy_max(n)

            run_iterations(act, iteration)

        @block.vector
        def _(dve):
            def settle(ins, done, value):
                ins.then_inc(done, 1)
                dve.wait_ge(done, at(value))

            def split_lo(hi_ready, value, bank, hi, lo, done, bias=None):
                dve.wait_ge(hi_ready, at(value))
                if bias is None:
                    ins = nc.vector.tensor_tensor(lo, shared[:, bank], hi.bitcast(F32), ALU.subtract)
                else:
                    ins = nc.vector.scalar_tensor_tensor(out=lo, in0=shared[:, bank], scalar=bias, in1=hi.bitcast(F32),
                                                         op0=ALU.add, op1=ALU.subtract)
                ins.then_inc(done, 1)

            def norm_stats(which, n, src):
                step = ln_step[which]
                for tt in range(TT):
                    nc.vector.bn_stats(stats[:, which, tt], src[:, tt])
                dve.drain()
                for tt in range(TT):
                    ins = nc.vector.bn_aggr(moments[:, which, tt], stats[:, which, tt])
                settle(ins, step, n.n + 1)
                nc.vector.tensor_scalar(var_eps[:, which], moments[:, which, :, 1], EPS, None, ALU.add)\
                    .then_inc(var_ready[which], 1)

            def norm_apply(which, n, src, dst, done):
                dve.wait_ge(rstd_ready[which], at(n.n + 1))
                for tt in range(TT):
                    ins = nc.vector.tensor_scalar(dst[:, tt], src[:, tt], moments[:, which, tt, 0:1],
                                                  rstd[:, which, tt:tt + 1], ALU.subtract, ALU.mult)
                ins.then_inc(done, 1)

            def norm_x(n, step):
                if step == 0:
                    dve.wait_ge(x_loaded[n.par], at(16 * (n.pair + 1)))
                    norm_stats(LN1, n, x_in[:, n.par])
                else:
                    wait(dve, h_ready, n.n)
                    norm_apply(LN1, n, x_in[:, n.par], xn, xn_ready)

            def split_h(n):
                split_lo(hT_hi_ready, n.n + 1, 1, hT_hi[:], hT_lo[:], hT_split)

            def split_qk(n):
                wait(dve, qk_stored, 64 * n.n)
                for side in range(2):
                    split_lo(qk_hi_ready, 2 * n.n + side + 1, side, qk_parts[:, side, 0], qk_parts[:, side, 1], qk_lo_ready,
                             bias=qk_bias[:, side:side + 1])

            def copy_v(n):
                dve.wait_ge(v_ready, at(n.n + 1))
                if n.first >= 2:
                    dve.wait_ge(pv_done, at(SETS * (n.n - 1)))
                nc.vector.tensor_tensor(values[n.par][:, :, :, 0:DH],
                                        shared[:, 1].rearrange("p (t h d) -> p t h d", t=TT, h=H),
                                        bv_row[:].rearrange("p (h d) -> p h d", h=H).unsqueeze(1)
                                        .broadcast_to([P, TT, H, DH]), ALU.add)\
                    .then_inc(values_ready, 1)

            def take_max(n, u):
                g, qt, i = u // (4 * TT), (u // 4) % TT, u % 4
                if u == 0:
                    wait(dve, max_split, n.n)
                dve.wait_ge(max_scores, at(UNITS * n.n + u + 1))
                nc.vector.tensor_reduce(neg_max[:, qt, i, g:g + 1], max_bank[:, u % 2], AX_X, ALU.max,
                                        negate=True).then_inc(max_taken, 1)

            def split_max(n):
                dve.wait_ge(max_taken, at(UNITS * (n.n + 1)))
                wait(dve, maxT_ready, n.n)
                settle(nc.vector.tensor_copy(max_parts[:, :, :, 0].bitcast(F32R), neg_max[:]), max_hi, n.n + 1)
                nc.vector.tensor_tensor(max_parts[:, :, :, 1].bitcast(F32R), neg_max[:], max_parts[:, :, :, 0],
                                        ALU.subtract).then_inc(max_split, 1)

            def normalise_o(b, g):
                dve.wait_ge(oq_ready, at(GROUPS * b.n + g + 1))
                wait(dve, o_ready, GROUPS * b.n + g - 1)
                heads = shared[:, 0].rearrange("p (t i c) -> p t i c", t=TT, i=4)
                settle(nc.vector.reciprocal(o_rcp[:, g % 2], heads[:, :, :, DH]), o_rcp_ready, GROUPS * b.n + g + 1)
                if g == 0:
                    wait(dve, o2T_ready, b.n)
                nc.vector.tensor_tensor(o[:].rearrange("p t (i g d) -> p t i g d", i=4, g=GROUPS)[:, :, :, g],
                                        heads[:, :, :, 0:DH],
                                        o_rcp[:, g % 2].unsqueeze(3).broadcast_to([P, TT, 4, DH]), ALU.mult)\
                    .then_inc(o_ready, 1)

            def residual(b):
                dve.wait_ge(wo_ready, at(b.n + 1))
                wait(dve, xn2T_ready, b.n)
                dve.wait_ge(h_ready, at(b.n + 1))
                dve.wait_ge(x_beta_ready, at(b.n + 1))
                ins = nc.vector.tensor_tensor(y[:], shared[:, 1].rearrange("p (t d) -> p t d", t=TT),
                                              h_bo[:, b.par], ALU.add)
                settle(ins, y_ready, b.n + 1)
                norm_stats(LN2, b, y)

            def finish_attention(b):
                norm_apply(LN2, b, y, y, yn_ready)
                dve.wait_ge(yn_ready, at(b.n + 1))
                if b.first >= 2:
                    dve.wait_ge(result_stored, at(16 * (b.n - 1)))
                rows = gamma_row[:].unsqueeze(1).broadcast_to([P, TT, P])
                settle(nc.vector.tensor_tensor(y[:], y[:], rows, ALU.mult), x2_step, 2 * b.n + 1)
                settle(nc.vector.tensor_tensor(x2[:, b.par], y[:], x_beta[:, b.par], ALU.add), x2_step, 2 * b.n + 2)

            def norm_x2(b, step):
                if step == 0:
                    norm_stats(LN3, b, x2[:, b.par])
                else:
                    norm_apply(LN3, b, x2[:, b.par], y, xn2_ready)

            def score_groups(b):
                st = ROUTE_STEPS * b.n
                dve.wait_ge(logits_exp, at(b.n + 1))
                settle(nc.vector.tensor_scalar(r_den[:], r_exp[:], 1.0, None, ALU.add), route_step, st + 1)
                settle(nc.vector.reciprocal(r_sig[:], r_den[:]), route_step, st + 2)
                settle(nc.vector.tensor_tensor(r_sc[:], r_sig[:], route_bias[:].unsqueeze(1)
                                               .broadcast_to([P, TT, E]), ALU.add), route_step, st + 3)
                fours = r_sc[:].rearrange("p t (g a c) -> p (t g) a c", a=2, c=2)
                nc.vector.tensor_tensor(r_max[:], fours[:, :, :, 0], fours[:, :, :, 1], ALU.max).then_inc(route_step, 1)
                nc.vector.tensor_tensor(r_min[:], fours[:, :, :, 0], fours[:, :, :, 1], ALU.min).then_inc(route_step, 1)
                dve.wait_ge(route_step, at(st + 5))
                nc.vector.tensor_tensor(r_own[:], r_max[:], r_min[:], ALU.add).then_inc(route_step, 1)
                nc.vector.tensor_tensor(r_two[:, :, 0], r_max[:, :, 0], r_max[:, :, 1], ALU.add).then_inc(route_step, 1)
                dve.wait_ge(route_step, at(st + 7))
                settle(nc.vector.tensor_tensor(r_two[:, :, 1], r_own[:, :, 0], r_own[:, :, 1], ALU.max), route_step, st + 8)
                settle(nc.vector.tensor_tensor(r_grp[:].rearrange("p t g -> p (t g)"), r_two[:, :, 0], r_two[:, :, 1],
                                               ALU.max), route_step, st + 9)

            def open_groups(b):
                st = ROUTE_STEPS * b.n
                others = r_grp[:].unsqueeze(2).broadcast_to([P, TT, EG, EG])
                own = r_grp[:].unsqueeze(3).broadcast_to([P, TT, EG, EG])
                nc.vector.tensor_tensor(r_gt[:], others, own, ALU.is_gt).then_inc(route_step, 1)
                settle(nc.vector.tensor_tensor(r_eq[:], others, own, ALU.is_equal), route_step, st + 11)
                settle(nc.vector.tensor_tensor(r_eq[:], r_eq[:], ties[:].unsqueeze(1).broadcast_to([P, TT, EG, EG]),
                                               ALU.mult), route_step, st + 12)
                settle(nc.vector.tensor_tensor(r_gt[:], r_gt[:], r_eq[:], ALU.add), route_step, st + 13)
                settle(nc.vector.tensor_reduce(r_rank[:], r_gt[:], AX_X, ALU.add), route_step, st + 14)
                settle(nc.vector.tensor_scalar(r_open[:], r_rank[:], 4.0, None, ALU.is_lt), route_step, st + 15)

            def route_experts(b):
                group = lambda a: a[:].rearrange("p t (g e) -> p (t g) e", g=EG)
                nc.vector.tensor_tensor(group(r_masked), group(r_sc),
                                               r_open[:].rearrange("p t g -> p (t g)").unsqueeze(2)
                                               .broadcast_to([P, TT * EG, E // EG]), ALU.mult).then_inc(route_step, 1)
                dve.drain()
                for tt in range(TT):
                    nc.vector.max(r_top[:, tt], r_masked[:, tt])
                dve.drain()
                for tt in range(TT):
                    nc.vector.match_replace(r_rest[:, tt], r_top[:, tt], r_masked[:, tt], -3.0e38)
                dve.drain()
                settle(nc.vector.tensor_tensor(r_sel[:], r_rest[:], r_masked[:], ALU.not_equal), comb_step, 5 * b.n + 1)
                settle(nc.vector.tensor_tensor(r_w[:], r_sel[:], r_sig[:], ALU.mult), comb_step, 5 * b.n + 2)
                settle(nc.vector.tensor_reduce(r_sum[:, 0], r_w[:], AX_X, ALU.add), comb_step, 5 * b.n + 3)
                settle(nc.vector.tensor_scalar(r_sum[:, 1], r_sum[:, 0], 1e-20, None, ALU.add), comb_step, 5 * b.n + 4)
                settle(nc.vector.reciprocal(r_sum[:, 2], r_sum[:, 1]), comb_step, 5 * b.n + 5)
                wait(dve, combT_ready, b.n)
                nc.vector.scalar_tensor_tensor(out=comb[:], in0=r_w[:], scalar=ROUTE_SCALE / 2,
                                               in1=r_sum[:, 2].unsqueeze(2).broadcast_to([P, TT, E]),
                                               op0=ALU.mult, op1=ALU.mult).then_inc(comb_ready, 1)

            def silu(f, k):
                dve.wait_ge(tanh_done, at(BLOCKS * f.n + k + 1))
                slot = (k + f.par) % 2
                wait(dve, act_done, BLOCKS * f.n + k - 1)
                nc.vector.scalar_tensor_tensor(out=f_silu[:, slot], in0=f_tanh[:, slot], scalar=1.0, in1=shared[:, 0],
                                               op0=ALU.add, op1=ALU.mult)\
                    .then_inc(silu_done, 1)

            def finish(f):
                dve.wait_ge(ffn_ready, at(f.n + 1))
                nc.vector.tensor_tensor(x2[:, f.par], shared[:, 1].rearrange("p (t d) -> p t d", t=TT), x2[:, f.par],
                                        ALU.add).then_inc(result_ready, 1)

            norm_x(Batch(0), 0)
            norm_x(Batch(0), 1)
            nc.vector.memset(out_bank[:], 0.0).then_inc(out_bank_set, 1)
            for i in range(2):
                nc.vector.memset(k_stack[i][:].bitcast(F32), 1.0).then_inc(ones_set, 1)
            dve.wait_ge(w_hi_ready, 2)
            nc.vector.tensor_tensor(w_lo[:], w_raw[:], w_hi[:].bitcast(F32), ALU.subtract).then_inc(w_split, 1)
            nc.vector.tensor_tensor(gate_lo[:], gate_raw[:], gate_hi[:].bitcast(F32), ALU.subtract).then_inc(w_split, 1)
            split_h(Batch(0))
            split_qk(Batch(0))
            dve.wait_ge(values_set, 2)
            copy_v(Batch(0))
            for u in range(UNITS):
                take_max(Batch(0), u)
                if u in (15, 19):
                    norm_x(Batch(1), (u - 15) // 4)
            split_max(Batch(0))
            split_h(Batch(1))
            split_qk(Batch(1))

            def iteration(t):
                n, p, f2 = t.plus(1), t.plus(-1), t.plus(-2)
                b, q = t, t.plus(2)
                for s in range(SLOTS):
                    if s == 1 and n.exists:
                        copy_v(n)
                    if s == 13 and q.exists:
                        split_h(q)
                    if s == 15 and q.exists:
                        split_qk(q)
                    if s == 1 and q.exists:
                        norm_x(q, 0)
                    if s in (6, 10, 14) and b.exists:
                        normalise_o(b, (s - 6) // 4)
                    if p.exists:
                        if s == 2:
                            normalise_o(p, GROUPS - 1)
                        if s == 3:
                            split_lo(o2T_hi_ready, p.n + 1, 1, o2T_hi[:], o2T_lo[:], o2T_split)
                        if s == 4:
                            residual(p)
                        if s == 5:
                            norm_x2(p, 0)
                        if s == 6:
                            split_lo(xn2T_hi_ready, p.n + 1, 1, xn2T_hi[:, p.par], xn2T_lo[:, p.par], xn2T_split)
                    if s == 12 and f2.exists:
                        finish(f2)
                    if s == 14 and n.exists:
                        split_max(n)
                    work = [(t.plus(-back), k) for k, back in FFN_SLOTS[s] if t.plus(-back).exists]
                    for j in range(4):
                        for u in max_tiles(s, j) if n.exists else ():
                            take_max(n, u)
                        if p.exists:
                            if (s, j) == (4, 0):
                                finish_attention(p)
                            if (s, j) == (5, 0):
                                norm_x2(p, 1)
                            if (s, j) == (7, 0):
                                score_groups(p)
                            if (s, j) == (7, 2):
                                open_groups(p)
                            if (s, j) == (8, 0):
                                route_experts(p)
                        if (s, j) == (1, 1) and q.exists:
                            norm_x(q, 1)
                        if j in (1, 3) and j // 2 < len(work):
                            silu(*work[j // 2])

            run_iterations(dve, iteration)

        @block.gpsimd
        def _(pool):
            def power(which, n):
                pool.wait_ge(var_ready[which], at(n.n + 1))
                wait(pool, (xn_ready, yn_ready, xn2_ready)[which], n.n)
                nc.gpsimd.tensor_tensor(rstd[:, which], var_eps[:, which], minus_half[:], ALU.pow)\
                    .then_inc(rstd_ready[which], 1)

            def add_positions(n):
                pool.wait_ge(xn_ready, at(n.n + 1))
                wait(pool, hT_ready, n.n)
                wait(pool, x_beta_ready, n.n)
                nc.gpsimd.tensor_tensor(h[:], xn[:], pos[:], ALU.add).then_inc(h_ready, 1)

            def add_biases(n):
                pool.wait_ge(h_ready, at(n.n + 1))
                if n.first >= 2:
                    pool.wait_ge(x2_step, at(2 * (n.n - 1)))
                row = lambda a: a[:].unsqueeze(1).broadcast_to([P, TT, P])
                nc.gpsimd.tensor_tensor(h_bo[:, n.par], h[:], row(bo_row), ALU.add).then_inc(h_bo_ready, 1)
                nc.gpsimd.tensor_tensor(x_beta[:, n.par], x_in[:, n.par], row(beta_row), ALU.add)\
                    .then_inc(x_beta_ready, 1)

            def gated_products(f, k):
                up = f_up[:, (k + f.par) % 2]
                pool.wait_ge(up_copied, at(BLOCKS * f.n + k + 1))
                if k > 0:
                    if (k - 1) % 4 == 0:
                        pool.wait_ge(comb_loaded[(k - 1) // 4], at(32 * (f.n + 1)))
                    nc.gpsimd.tensor_tensor(up, up, comb_all[:, (k - 1) % 8], ALU.mult).then_inc(weighed, 1)
                    pool.wait_ge(weighed, at((BLOCKS - 1) * f.n + k))
                pool.wait_ge(silu_done, at(BLOCKS * f.n + k + 1))
                wait(pool, down_done, BLOCKS * f.n + k - 2 if k > 3 else BLOCKS * f.n if k else BLOCKS * (f.n - 1) + 1)
                nc.gpsimd.tensor_tensor(f_act[:, 1 + k % 3 if k else 0], f_silu[:, (k + f.par) % 2], up, ALU.mult)\
                    .then_inc(act_done, 1)

            nc.gpsimd.memset(minus_half[:], -0.5).then_inc(exponent_set, 1)
            pool.wait_ge(exponent_set, 1)
            power(LN1, Batch(0))
            for i in range(2):
                nc.gpsimd.memset(values[i][:, :, :, DH:DH + 1], 1.0).then_inc(values_set, 1)
            pool.wait_ge(consts_loaded, N_CONSTS)
            add_positions(Batch(0))
            add_biases(Batch(0))
            power(LN1, Batch(1))
            add_positions(Batch(1))
            pool.wait_ge(experts_hi, 2)
            for side in range(2):
                nc.gpsimd.tensor_tensor(wgu_lo[:, side].rearrange("p k m -> p (k m)"), raw_experts[side],
                                        wgu_hi[:, side].rearrange("p k m -> p (k m)").bitcast(F32), ALU.subtract)\
                    .then_inc(experts_split, 1)

            def iteration(t):
                n, p = t.plus(1), t.plus(-1)
                for s in range(SLOTS):
                    if s == 4 and p.exists:
                        power(LN2, p)
                    if s == 5 and p.exists:
                        power(LN3, p)
                    if s == 6 and n.exists:
                        add_biases(n)
                    if s == 1 and t.plus(2).exists:
                        power(LN1, t.plus(2))
                    if s == 7 and t.plus(2).exists:
                        add_positions(t.plus(2))
                    for k, back in FFN_SLOTS[s]:
                        f = t.plus(-back)
                        if f.exists:
                            gated_products(f, k)

            run_iterations(pool, iteration)


def positional_encoding():
    import numpy as np

    position = np.arange(T, dtype=np.float32)[:, None]
    rate = np.exp(np.arange(0, P, 2, dtype=np.float32) * np.float32(-np.log(10000.0) / P)).astype(np.float32)
    table = np.zeros((T, P), np.float32)
    table[:, 0::2] = np.sin(position * rate)
    table[:, 1::2] = np.cos(position * rate)
    return table


def kernel(**inputs):
    import numpy as np
    import concourse.bacc as bacc
    from concourse import mybir as mb
    from concourse.bass_utils import run_bass_kernel_spmd

    a = {k: np.asarray(v) for k, v in inputs.items()}
    attn = lambda k: a[f"L0_attn_{k}"]
    ffn = lambda k: a[f"L0_ffn_{k}"]
    gate_in = np.concatenate([ffn("sh_gate").T, ffn("w_gate").reshape(E * EI, P).T], axis=1)
    up_in = np.concatenate([ffn("sh_up").T, ffn("w_up").reshape(E * EI, P).T], axis=1)
    down = np.concatenate([ffn("sh_down").T, ffn("w_down").transpose(0, 2, 1).reshape(E * EI, P)], axis=0)
    arrays = {
        "x": attn("x"), "wq": attn("Wq"), "wk": attn("Wk"), "wv": attn("Wv"), "wo": attn("Wo"),
        "bq": attn("bq"), "bk": attn("bk"), "bv": attn("bv"), "bo": attn("bo"),
        "gamma": attn("gamma"), "beta": attn("beta"),
        "gate_wT": ffn("gate_w").T, "gate_bias": ffn("gate_bias"),
        "w_gateT": gate_in, "w_upT": up_in,
        "w_downT": down.reshape(BLOCKS, P, P).transpose(1, 0, 2),
        "pe_table": positional_encoding().reshape(TT, P, P).transpose(1, 0, 2),
        "identity": np.eye(P, dtype=np.float32),
        "tie_mask": np.broadcast_to(np.tril(np.ones((EG, EG), np.float32), -1), (P, EG, EG)),
    }
    nc = bacc.Bacc("TRN2", target_bir_lowering=False, num_devices=1)
    arrays = {f"in_{k}": np.ascontiguousarray(v) for k, v in arrays.items()}
    args = [nc.dram_tensor(k, v.shape, mb.dt.from_np(v.dtype), kind="ExternalInput").ap() for k, v in arrays.items()]
    out = nc.dram_tensor("out_y", (B, T, P), mb.dt.float32, kind="ExternalOutput").ap()
    build_layer(nc, *args, out)
    r = run_bass_kernel_spmd(nc, [arrays], core_ids=[0])
    return r.results[0]["out_y"]
```

```python
from contextlib import ExitStack

import concourse.bass as bass
from concourse import mybir

F32 = mybir.dt.float32
F32R = mybir.dt.float32r
ALU = mybir.AluOpType
ACT = mybir.ActivationFunctionType
AX_X = mybir.AxisListType.X

P = 128
B = 8
T = 512
TT = T // P
H = 16
DH = P // H
GROUPS = 4
E = 32
EG = 8
EI = 64
BLOCKS = 1 + E * EI // P
STACK = 3 * DH
UNITS = H * TT
SETS = UNITS // 4
SLOTS = 16
CHUNKS = 4
EPS = 1e-5
ROUTE_SCALE = 2.5
ROUTE_STEPS = 12
LN1, LN2, LN3 = range(3)
MAX_PARTS = (range(3), range(3, 4), range(0, 1), range(1, 2), range(2, 3))
FIRST_PARTS = (2, 3, 4, 1)
WARM_UP = 12
WARM_QUARTER = (3, 1, 2)
FIRST_TILES = 32
FIRST_QUARTERS = (2, 1, 2, 2, 1)

MAX_TILES = [(1, 1, 1, 1), (1, 1, 0, 0), (1, 2, 1, 2), (1, 2, 1, 2), (0, 0, 0, 0), (0, 0, 1, 1), (1, 1, 1, 2),
             (0, 0, 0, 0), (0, 0, 0, 0), (1, 2, 1, 2), (1, 2, 1, 2), (1, 2, 1, 2), (1, 2, 1, 2), (1, 2, 1, 1),
             (1, 2, 1, 1), (1, 2, 1, 1)]
LATE_TILES = sum(map(sum, MAX_TILES[:2]))
assert sum(map(sum, MAX_TILES)) == UNITS
FFN_SLOTS = [[(7 + s, 2)] for s in range(10)] + [[(s, 1)] for s in range(5)] + [[(5, 1), (6, 1)]]


def max_tiles(t, s, j):
    if t.first == 0:
        opening = len(FIRST_QUARTERS)
        if s < opening:
            first = FIRST_TILES + 4 * sum(FIRST_QUARTERS[:s]) + j * FIRST_QUARTERS[s]
            return t, list(range(first, first + FIRST_QUARTERS[s]))
        quarters, tiles = 4 * (SLOTS - opening), UNITS - LATE_TILES
        q = 4 * (s - opening) + j
        return t.plus(1), list(range(-(-tiles * q // quarters), -(-tiles * (q + 1) // quarters)))
    first = sum(sum(quarters) for quarters in MAX_TILES[:s]) + sum(MAX_TILES[s][:j])
    batch, shift = (t, UNITS - LATE_TILES) if s < 2 else (t.plus(1), -LATE_TILES)
    return batch, [first + shift + i for i in range(MAX_TILES[s][j])] if batch.exists else []


def max_slots(t):
    return ((3, 3, 4), (5, 6, 1)) if t.first == 0 else ((2, 2, 1),) if t.exists else ()


class Count:

    def __init__(self, trip, scale, base):
        self.trip, self.scale, self.base = trip, scale, base

    def __add__(self, k):
        return Count(self.trip, self.scale, self.base + k)

    def __sub__(self, k):
        return self + -k

    def __mul__(self, k):
        return Count(self.trip, self.scale * k, self.base * k)

    __rmul__ = __mul__


def at(count):
    return count.trip * count.scale + count.base if isinstance(count, Count) else count


class Batch:

    def __init__(self, first, trip=None):
        self.first, self.trip, self.par = first, trip, first % 2
        self.n = first if trip is None else Count(trip, 2, first)
        self.pair = first // 2 if trip is None else Count(trip, 1, first // 2)
        self.exists = 0 <= first < B

    def plus(self, k):
        return Batch(self.first + k, self.trip)


def wait(eng, sem, count):
    if isinstance(count, Count) or count > 0:
        eng.wait_ge(sem, at(count))


def earlier(n, part):
    return n.n if part == 1 else n.n - 1 if part == 0 else 0


def build_layer(nc, x, wq, wk, wv, wo, bq, bk, bv, bo, gamma, beta, gate_wT, gate_bias, w_gateT,
                w_upT, w_downT, pe_table, identity, out):
    with ExitStack() as ctx:
        def sb(name, shape, dt=F32):
            return ctx.enter_context(nc.sbuf_tensor(name, shape, dt))

        def ps(name, shape):
            return ctx.enter_context(nc.psum_tensor(name, shape, F32))

        def sem(name):
            return ctx.enter_context(nc.semaphore(name))

        ident = sb("ident", [P, P])
        pos = sb("pos", [P, TT, P])
        w_hi = sb("w_hi", [P, 4, P], F32R)
        w_lo = sb("w_lo", [P, 4, P], F32R)
        gate_raw = sb("gate_raw", [P, E])
        gate_hi = sb("gate_hi", [P, E], F32R)
        gate_lo = sb("gate_lo", [P, E], F32R)
        wgu_hi = sb("wgu_hi", [P, 2, BLOCKS, P], F32R)
        wgu_lo = sb("wgu_lo", [P, 2, BLOCKS, P], F32R)
        w_down = sb("w_down", [P, BLOCKS, P])
        qk_bias = sb("qk_bias", [P, 2])
        bv_row = sb("bv_row", [P, P])
        bo_row = sb("bo_row", [P, P])
        gamma_row = sb("gamma_row", [P, P])
        beta_row = sb("beta_row", [P, P])
        route_bias = sb("route_bias", [P, E])
        minus_half = sb("minus_half", [P, TT])

        x_in = sb("x_in", [P, 2, TT, P])
        x_beta = sb("x_beta", [P, 2, TT, P])
        xn = sb("xn", [P, TT, P])
        h = sb("h", [P, TT, P])
        h_bo = sb("h_bo", [P, 2, TT, P])
        hT_hi = sb("hT_hi", [P, T], F32R)
        hT_lo = sb("hT_lo", [P, T], F32R)
        qk_parts = sb("qk_parts", [P, 2, 2, T], F32R)
        q_stack = [sb(f"q_stack{i}", [P, GROUPS, T], F32R) for i in range(2)]
        k_stack = [sb(f"k_stack{i}", [P, GROUPS, T], F32R) for i in range(2)]
        values = [sb(f"values{i}", [P, TT, H, DH + 1]) for i in range(2)]
        neg_max = sb("neg_max", [P, TT, GROUPS, 4])
        max_parts = sb("max_parts", [P, TT, GROUPS, 4, 2])
        maxT = [sb(f"maxT{part}", [8 * len(MAX_PARTS[part]), T])[:] for part in range(2)]
        probs = sb("probs", [P, 8, T])
        oT = sb("oT", [P, 2, T])
        o_rcp = sb("o_rcp", [P, 2, TT, 4])
        o = sb("o", [P, TT, P])
        o2T_hi = sb("o2T_hi", [P, T], F32R)
        o2T_lo = sb("o2T_lo", [P, T], F32R)
        y = sb("y", [P, TT, P])
        x2 = sb("x2", [P, 2, TT, P])
        xn2T_hi = sb("xn2T_hi", [P, 2, T], F32R)
        xn2T_lo = sb("xn2T_lo", [P, 2, T], F32R)
        stats = sb("stats", [P, 3, TT, 6])
        moments = sb("moments", [P, 3, TT, 2])
        var_eps = sb("var_eps", [P, 3, TT])
        rstd = sb("rstd", [P, 3, TT])
        r_exp = sb("r_exp", [P, TT, E])
        r_den = sb("r_den", [P, TT, E])
        r_sig = sb("r_sig", [P, TT, E])
        r_sc = sb("r_sc", [P, TT, E])
        r_max = sb("r_max", [P, TT * EG, 2])
        r_min = sb("r_min", [P, TT * EG, 2])
        r_own = sb("r_own", [P, TT * EG, 2])
        r_two = sb("r_two", [P, TT * EG, 2])
        r_grp = sb("r_grp", [P, TT, EG])
        r_ranked = sb("r_ranked", [P, TT, EG])
        r_best = sb("r_best", [P, TT, EG])
        r_closed = sb("r_closed", [P, TT, EG])
        r_open = sb("r_open", [P, TT, EG])
        r_masked = sb("r_masked", [P, TT, E])
        r_top = sb("r_top", [P, TT, 8])
        r_rest = sb("r_rest", [P, TT, E])
        r_sel = sb("r_sel", [P, TT, E])
        r_w = sb("r_w", [P, TT, E])
        r_sum = sb("r_sum", [P, 3, TT])
        comb = sb("comb", [P, TT, E])
        combT = sb("combT", [E, T])
        comb_all = sb("comb_all", [P, 8, T])
        f_tanh = sb("f_tanh", [P, 2, T])
        f_silu = sb("f_silu", [P, 2, T])
        f_up = sb("f_up", [P, 2, T])
        f_act = sb("f_act", [P, 4, T])
        ffnT = sb("ffnT", [P, T])

        max_bank = ps("max_bank", [P, 2, T])
        exp_bank = ps("exp_bank", [P, 2, T])
        out_bank = ps("out_bank", [P, T])
        down_bank = ps("down_bank", [P, T])
        shared = ps("shared", [P, 2, T])

        maxT += [f_act[0:8, i] for i in range(3)]
        w_raw = y
        raw_experts = [comb_all[:].rearrange("p a b -> p (a b)")[:, 0:BLOCKS * P],
                       probs[:].rearrange("p a b -> p (a b)")[:, 0:BLOCKS * P]]

        qk_scratch = nc.dram_tensor("qk_scratch", (2, 2, P, 3, T), F32).ap()
        max_scratch = nc.dram_tensor("max_scratch", (2, 4 * 2 * GROUPS, T), F32).ap()
        comb_scratch = nc.dram_tensor("comb_scratch", (2, E, T), F32).ap()

        consts_loaded = sem("consts_loaded")
        weights_loaded = sem("weights_loaded")
        experts_loaded = sem("experts_loaded")
        down_loaded = sem("down_loaded")
        ones_set = sem("ones_set")
        values_set = sem("values_set")
        out_bank_set = sem("out_bank_set")
        h_bo_ready = sem("h_bo_ready")
        comb_step = sem("comb_step")
        exponent_set = sem("exponent_set")
        w_hi_ready = sem("w_hi_ready")
        w_split = sem("w_split")
        experts_hi = sem("experts_hi")
        experts_split = sem("experts_split")
        x_loaded = [sem(f"x_loaded{i}") for i in range(2)]
        ln_step = [sem(f"ln_step{i}") for i in range(3)]
        var_ready = [sem(f"var_ready{i}") for i in range(3)]
        rstd_ready = [sem(f"rstd_ready{i}") for i in range(3)]
        xn_ready = sem("xn_ready")
        h_ready = sem("h_ready")
        x_beta_ready = sem("x_beta_ready")
        hT_ready = sem("hT_ready")
        hT_hi_ready = sem("hT_hi_ready")
        hT_split = sem("hT_split")
        qk_ready = sem("qk_ready")
        qk_hi_ready = sem("qk_hi_ready")
        qk_lo_ready = sem("qk_lo_ready")
        qk_stored = sem("qk_stored")
        stack_loaded = sem("stack_loaded")
        v_ready = sem("v_ready")
        values_ready = sem("values_ready")
        max_scores = sem("max_scores")
        max_taken = sem("max_taken")
        max_hi = [sem(f"max_hi{part}") for part in range(5)]
        max_split = [sem(f"max_split{part}") for part in range(5)]
        maxT_ready = [sem(f"maxT_ready{part}") for part in range(5)]
        maxT_copied = [sem(f"maxT_copied{part}") for part in range(5)]
        max_stored = [sem(f"max_stored{part}") for part in range(5)]
        max_loaded = [sem(f"max_loaded{part}") for part in range(5)]
        scores_ready = sem("scores_ready")
        exp_done = sem("exp_done")
        pv_done = sem("pv_done")
        oT_copied = sem("oT_copied")
        oq_ready = sem("oq_ready")
        o_rcp_ready = sem("o_rcp_ready")
        o_ready = sem("o_ready")
        o2T_ready = sem("o2T_ready")
        o2T_hi_ready = sem("o2T_hi_ready")
        o2T_split = sem("o2T_split")
        wo_ready = sem("wo_ready")
        y_ready = sem("y_ready")
        yn_ready = sem("yn_ready")
        x2_step = sem("x2_step")
        xn2_ready = sem("xn2_ready")
        xn2T_ready = sem("xn2T_ready")
        xn2T_hi_ready = sem("xn2T_hi_ready")
        xn2T_split = sem("xn2T_split")
        logits_ready = sem("logits_ready")
        logits_exp = sem("logits_exp")
        route_step = sem("route_step")
        best_filled = sem("best_filled")
        comb_ready = sem("comb_ready")
        combT_ready = sem("combT_ready")
        combT_copied = sem("combT_copied")
        comb_stored = sem("comb_stored")
        comb_loaded = [sem(f"comb_loaded{i}") for i in range(CHUNKS)]
        gate_ready = sem("gate_ready")
        up_ready = sem("up_ready")
        tanh_done = sem("tanh_done")
        silu_done = sem("silu_done")
        up_copied = sem("up_copied")
        weighed = sem("weighed")
        act_done = sem("act_done")
        down_done = sem("down_done")
        ffnT_copied = sem("ffnT_copied")
        ffn_ready = sem("ffn_ready")
        result_ready = sem("result_ready")
        result_stored = sem("result_stored")

        x_view = x.rearrange("b (t p) d -> b p t d", p=P)
        out_view = out.rearrange("b (t p) d -> b p t d", p=P)
        N_CONSTS = 16 * 10
        LOOP_FROM, LOOP_TRIPS = 2, 2

        def run_iterations(eng, iteration, start_loop=None, end_loop=None):
            for t in range(LOOP_FROM):
                iteration(Batch(t))
            with eng.Fori(0, LOOP_TRIPS) as trip:
                eng.get_value_cache().nocache = True
                if start_loop:
                    start_loop(Batch(LOOP_FROM, trip))
                for u in range(2):
                    iteration(Batch(LOOP_FROM + u, trip))
            if end_loop:
                end_loop(Batch(LOOP_FROM + 2 * LOOP_TRIPS))
            for t in range(LOOP_FROM + 2 * LOOP_TRIPS, B + 2):
                iteration(Batch(t))

        def expert_banks(f, k, side, tail):
            own = 2 if tail and (k + f.par) % 2 else 0
            return own + side, (exp_bank if own else shared)[:, side]

        block = ctx.enter_context(nc.Block())

        @block.sync
        def _(sp):
            def store_qk(n):
                scratch = qk_scratch[n.par]
                sp.wait_ge(qk_lo_ready, at(2 * n.n + 1))
                sp.dma_start(scratch[0, :, 1:3], qk_parts[:, 0].bitcast(F32)).then_inc(qk_stored, 16)
                sp.wait_ge(qk_hi_ready, at(2 * n.n + 2))
                sp.dma_start(scratch[:, :, 0].rearrange("s p n -> p s n"), qk_parts[:, :, 0].bitcast(F32))\
                    .then_inc(qk_stored, 16)
                sp.dma_start(scratch[1, :, 2], qk_parts[:, 1, 0].bitcast(F32)).then_inc(qk_stored, 16)
                sp.wait_ge(qk_lo_ready, at(2 * n.n + 2))
                sp.dma_start(scratch[1, :, 1], qk_parts[:, 1, 1].bitcast(F32)).then_inc(qk_stored, 16)

            def load_stacks(n):
                wait(sp, scores_ready, UNITS * (n.n - 1))
                sp.wait_ge(qk_stored, at(64 * n.n + 64))
                for side, stack in enumerate((q_stack, k_stack)):
                    rows = qk_scratch[n.par, side].rearrange("(i g d) j n -> i (d j) g n", g=GROUPS, d=DH)
                    for i in range(4):
                        row = 32 * i
                        sp.dma_start(stack[n.par][row:row + STACK].bitcast(F32), rows[i]).then_inc(stack_loaded, 16)

            def stack_max(n, part):
                groups = slice(MAX_PARTS[part].start, MAX_PARTS[part].stop)
                sp.wait_ge(maxT_copied[part], at(earlier(n, part) + 1))
                sp.dma_start(max_scratch[n.par, 8 * groups.start:8 * groups.stop], maxT[part])\
                    .then_inc(max_stored[part], 16)
                sp.wait_ge(max_stored[part], at(16 * earlier(n, part) + 16))
                rows = max_scratch[n.par].rearrange("(g i a) n -> i a g n", i=4, a=2)
                for i in range(4):
                    row = 32 * i + STACK
                    sp.dma_start(q_stack[n.par][row:row + 2, groups].bitcast(F32), rows[i, :, groups])\
                        .then_inc(max_loaded[part], 16)

            def store_comb(f):
                sp.wait_ge(combT_copied, at(f.n + 1))
                sp.dma_start(comb_scratch[f.par], combT[:]).then_inc(comb_stored, 16)
                sp.wait_ge(comb_stored, at(16 * f.n + 16))

            def broadcast_comb(f, c):
                rows = comb_scratch[f.par].rearrange("(k a) n -> a k n", a=2)
                wait(sp, act_done, BLOCKS * f.n + 4 * c - 3 if c > 1 else BLOCKS * (f.n - 1) + 4 * c + 13)
                slot = 4 * (c % 2)
                for a in range(2):
                    src = rows[a, 4 * c:4 * c + 4].unsqueeze(0).broadcast_to([EI, 4, T])
                    sp.dma_start(comb_all[EI * a:EI * a + EI, slot:slot + 4], src).then_inc(comb_loaded[c], 16)

            def store_result(f):
                sp.wait_ge(result_ready, at(f.n + 1))
                sp.dma_start(out_view[at(f.n)], x2[:, f.par]).then_inc(result_stored, 16)

            for n in (Batch(0), Batch(1)):
                sp.dma_start(x_in[:, n.par], x_view[n.n]).then_inc(x_loaded[n.par], 16)
            for dst, src in ((ident[:], identity), (pos[:], pe_table),
                             (bv_row[:], bv.partition_broadcast(P)), (bo_row[:], bo.partition_broadcast(P)),
                             (gamma_row[:], gamma.partition_broadcast(P)),
                             (beta_row[:], beta.partition_broadcast(P)),
                             (route_bias[:], gate_bias.partition_broadcast(P)),
                             (gate_raw[:], gate_wT), (qk_bias[:, 0:1], bq.unsqueeze(1)),
                             (qk_bias[:, 1:2], bk.unsqueeze(1))):
                sp.dma_start(dst, src).then_inc(consts_loaded, 16)
            for n, w in enumerate((wq, wk, wv, wo)):
                sp.dma_start(w_raw[:, n], w).then_inc(weights_loaded, 16)
            for side, w in enumerate((w_gateT, w_upT)):
                sp.dma_start(raw_experts[side], w).then_inc(experts_loaded, 16)
            sp.dma_start(w_down[:], w_downT).then_inc(down_loaded, 16)
            sp.wait_ge(ones_set, 2)
            store_qk(Batch(0))
            load_stacks(Batch(0))
            stack_max(Batch(0), 2)
            store_qk(Batch(1))
            load_stacks(Batch(1))
            stack_max(Batch(0), 3)

            def iteration(t):
                if t.plus(-2).exists:
                    broadcast_comb(t.plus(-2), 3)
                for _, _, part in max_slots(t):
                    stack_max(t, part)
                if t.plus(-1).exists:
                    if t.first == 1:
                        sp.wait_ge(experts_split, 2)
                    store_comb(t.plus(-1))
                    broadcast_comb(t.plus(-1), 0)
                    broadcast_comb(t.plus(-1), 1)
                if t.plus(-2).exists:
                    store_result(t.plus(-2))
                if t.plus(2).exists:
                    store_qk(t.plus(2))
                if t.plus(1).exists:
                    stack_max(t.plus(1), 0)
                if t.plus(-1).exists:
                    broadcast_comb(t.plus(-1), 2)
                if t.plus(2).exists:
                    load_stacks(t.plus(2))

            run_iterations(sp, iteration)
            sp.wait_ge(result_stored, 16 * B)

        @block.tensor
        def _(pe):
            last_reader = [None, None, (exp_done, UNITS * B - 1), (exp_done, UNITS * B)]

            def claim(bank, done, value):
                if last_reader[bank]:
                    done_before, value_before = last_reader[bank]
                    pe.wait_ge(done_before, at(value_before))
                last_reader[bank] = (done, value)

            def products(dst, pairs, start=True, stop=True):
                for n, (left, right) in enumerate(pairs):
                    last = nc.tensor.matmul(dst, left, right, start=start and n == 0,
                                            stop=stop and n == len(pairs) - 1)
                return last

            def keep_clock(times):
                for _ in range(times):
                    nc.tensor.matmul(down_bank[:], wgu_hi[:, 0, 0], wgu_hi[:, 0, 0:4].rearrange("p k m -> p (k m)"),
                                     start=True, stop=True)

            def transpose_h(n):
                pe.wait_ge(h_ready, at(n.n + 1))
                claim(1, hT_split, n.n + 1)
                for tt in range(TT):
                    last = nc.tensor.transpose(shared[:, 1, tt * P:tt * P + P], h[:, tt], ident[:])
                last.then_inc(hT_ready, 1)

            def project_qk(n, side):
                pe.wait_ge(hT_split, at(n.n + 1))
                claim(1, qk_lo_ready, 2 * n.n + side + 1)
                products(shared[:, 1], [(w_hi[:, side], hT_hi[:]), (w_lo[:, side], hT_hi[:]),
                                        (w_hi[:, side], hT_lo[:])]).then_inc(qk_ready, 1)

            def project_v(n):
                claim(1, values_ready, n.n + 1)
                for tt in range(TT):
                    cols = slice(tt * P, tt * P + P)
                    last = products(shared[:, 1, cols], [(hT_hi[:, cols], w_hi[:, 2]), (hT_hi[:, cols], w_lo[:, 2]),
                                                         (hT_lo[:, cols], w_hi[:, 2])])
                last.then_inc(v_ready, 1)

            def max_unit(n, u):
                g, qt, i = u // (4 * TT), (u // 4) % TT, u % 4
                if u == 0:
                    pe.wait_ge(stack_loaded, at(16 * 8 * (n.n + 1)))
                wait(pe, max_taken, UNITS * n.n + u - 1)
                rows = slice(32 * i, 32 * i + STACK)
                nc.tensor.matmul(max_bank[:, u % 2], q_stack[n.par][rows, g, qt * P:qt * P + P],
                                 k_stack[n.par][rows, g, :], start=True, stop=True).then_inc(max_scores, 1)

            def transpose_max(n, part):
                pe.wait_ge(max_split[part], at(earlier(n, part) + 1))
                claim(0, maxT_copied[part], earlier(n, part) + 1)
                groups = slice(MAX_PARTS[part].start, MAX_PARTS[part].stop)
                rows = 8 * len(MAX_PARTS[part])
                for tt in range(TT):
                    last = nc.tensor.transpose(shared[0:rows, 0, tt * P:tt * P + P],
                                               max_parts[:, tt, groups].rearrange("p g i a -> p (g i a)"), ident[:])
                last.then_inc(maxT_ready[part], 1)

            def exp_unit(b, u):
                g, kt, i = u // (4 * TT), (u // 4) % TT, u % 4
                for part in FIRST_PARTS if b.first == 0 else (0, 1):
                    if u == 4 * TT * MAX_PARTS[part].start:
                        pe.wait_ge(max_loaded[part], at(64 * (earlier(b, part) + 1)))
                wait(pe, exp_done, UNITS * b.n + u - 1)
                rows = slice(32 * i, 32 * i + STACK + 2)
                nc.tensor.matmul(exp_bank[:, u % 2], k_stack[b.par][rows, g, kt * P:kt * P + P],
                                 q_stack[b.par][rows, g, :], start=True, stop=True).then_inc(scores_ready, 1)

            def value_set(b, s):
                g, kt = s // TT, s % TT
                if s == 0:
                    pe.wait_ge(values_ready, at(b.n + 1))
                if s == 0 and b.first == 0:
                    pe.wait_ge(out_bank_set, 1)
                if kt == 0:
                    wait(pe, oT_copied, GROUPS * b.n + g)
                pe.wait_ge(exp_done, at(UNITS * b.n + 4 * s + 4))
                for i in range(4):
                    last = nc.tensor.matmul(out_bank[32 * i:32 * i + DH + 1], values[b.par][:, kt, 4 * i + g, :],
                                            probs[:, (4 * s + i) % 8], start=(kt == 0), stop=(kt == TT - 1))
                last.then_inc(pv_done, 1)

            def transpose_o(b, g):
                pe.wait_ge(oT_copied, at(GROUPS * b.n + g + 1))
                claim(0, o_ready, GROUPS * b.n + g + 1)
                for tt in range(TT):
                    cols = slice(tt * P, tt * P + P)
                    last = nc.tensor.transpose(shared[:, 0, cols], oT[:, g % 2, cols], ident[:])
                last.then_inc(oq_ready, 1)

            def transpose_o2(b):
                pe.wait_ge(o_ready, at(GROUPS * (b.n + 1)))
                claim(1, o2T_split, b.n + 1)
                for tt in range(TT):
                    last = nc.tensor.transpose(shared[:, 1, tt * P:tt * P + P], o[:, tt], ident[:])
                last.then_inc(o2T_ready, 1)

            def project_o(b):
                pe.wait_ge(o2T_split, at(b.n + 1))
                claim(1, y_ready, b.n + 1)
                for tt in range(TT):
                    cols = slice(tt * P, tt * P + P)
                    last = products(shared[:, 1, cols], [(o2T_hi[:, cols], w_hi[:, 3]), (o2T_hi[:, cols], w_lo[:, 3]),
                                                         (o2T_lo[:, cols], w_hi[:, 3])])
                last.then_inc(wo_ready, 1)

            def transpose_xn2(b):
                pe.wait_ge(xn2_ready, at(b.n + 1))
                claim(1, xn2T_split, b.n + 1)
                for tt in range(TT):
                    last = nc.tensor.transpose(shared[:, 1, tt * P:tt * P + P], y[:, tt], ident[:])
                last.then_inc(xn2T_ready, 1)

            def route(b):
                pe.wait_ge(xn2T_split, at(b.n + 1))
                claim(1, logits_exp, b.n + 1)
                hi, lo = xn2T_hi[:, b.par], xn2T_lo[:, b.par]
                for tt in range(TT):
                    cols = slice(tt * P, tt * P + P)
                    last = products(shared[:, 1, tt * E:tt * E + E], [(hi[:, cols], gate_hi[:]), (hi[:, cols], gate_lo[:]),
                                                                      (lo[:, cols], gate_hi[:])])
                last.then_inc(logits_ready, 1)

            def transpose_comb(b):
                pe.wait_ge(comb_ready, at(b.n + 1))
                claim(1, combT_copied, b.n + 1)
                for tt in range(TT):
                    last = nc.tensor.transpose(shared[0:E, 1, tt * P:tt * P + P], comb[:, tt], ident[:])
                last.then_inc(combT_ready, 1)

            def expert_in(f, k, side, tail):
                if f.first == 0 and k == 0 and side == 0:
                    pe.wait_ge(experts_split, 2)
                bank, dst = expert_banks(f, k, side, tail)
                claim(bank, up_copied if side else silu_done, BLOCKS * f.n + k + 1)
                hi, lo = xn2T_hi[:, f.par], xn2T_lo[:, f.par]
                products(dst, [(wgu_hi[:, side, k], hi), (wgu_lo[:, side, k], hi), (wgu_hi[:, side, k], lo)]
                         )\
                    .then_inc(up_ready if side else gate_ready, 1)

            def expert_out(f, k):
                if k == 0:
                    if f.first == 0:
                        pe.wait_ge(down_loaded, 16)
                    wait(pe, ffnT_copied, f.n)
                pe.wait_ge(act_done, at(BLOCKS * f.n + k + 1))
                hidden = f_act[:, 1 + k % 3 if k else 0]
                nc.tensor.matmul(down_bank[:], w_down[:, k], hidden, start=(k == 0),
                                 stop=(k == BLOCKS - 1)).then_inc(down_done, 1)

            def transpose_ffn(f):
                pe.wait_ge(ffnT_copied, at(f.n + 1))
                claim(1, result_ready, f.n + 1)
                for tt in range(TT):
                    cols = slice(tt * P, tt * P + P)
                    last = nc.tensor.transpose(shared[:, 1, cols], ffnT[:, cols], ident[:])
                last.then_inc(ffn_ready, 1)

            pe.wait_ge(consts_loaded, N_CONSTS)
            transpose_h(Batch(0))
            pe.wait_ge(w_split, 2)
            project_qk(Batch(0), 0)
            project_qk(Batch(0), 1)
            project_v(Batch(0))
            for u in range(FIRST_TILES):
                max_unit(Batch(0), u)
                if u == 17:
                    transpose_max(Batch(0), 2)
                if u == 19:
                    transpose_h(Batch(1))
                if u in (23, 25):
                    project_qk(Batch(1), (u - 23) // 2)
            pe.wait_ge(experts_hi, 2)
            keep_clock(WARM_UP)
            transpose_max(Batch(0), 3)

            def iteration(t):
                b, n, p, f2 = t, t.plus(1), t.plus(-1), t.plus(-2)
                tail = t.first >= B
                for s in range(SLOTS):
                    work = [(t.plus(-back), k) for k, back in FFN_SLOTS[s] if t.plus(-back).exists]
                    for j in range(4):
                        if b.exists:
                            exp_unit(b, 4 * s + j)
                        owner, tiles = max_tiles(t, s, j)
                        for u in tiles[:1]:
                            max_unit(owner, u)
                        if t.first == 0 or t.first == 1 and not work:
                            keep_clock(WARM_QUARTER[t.first + 1 if t.first or s >= len(FIRST_QUARTERS) else 0])
                        if len(work) == 2:
                            expert_in(*work[j // 2], j % 2, tail)
                        elif work and j in (0, 2):
                            expert_in(*work[0], j // 2, tail)
                        if j == 1 and s == 0 and p.exists:
                            value_set(p, SETS - 1)
                        if j == 1 and s > 0 and b.exists:
                            value_set(b, s - 1)
                        if (s, j) == (14, 2) and n.exists:
                            transpose_max(n, 0)
                        for _, slot, part in max_slots(b):
                            if (s, j) == (slot, 2):
                                transpose_max(b, part)
                        if s in (5, 9, 13) and j == 2 and b.exists:
                            transpose_o(b, (s - 5) // 4)
                        if (s, j) == (1, 2) and p.exists:
                            transpose_o(p, GROUPS - 1)
                        if tail:
                            if s == 15 and j in (1, 3) and p.exists:
                                expert_out(p, 3 + j // 2)
                            if s < 15 and j == 3:
                                for f, k in work:
                                    if k >= 2:
                                        expert_out(f, k - 2)
                                if s == 10 and f2.exists:
                                    expert_out(f2, BLOCKS - 2)
                        else:
                            if j == 1 and s == 15 and p.exists:
                                expert_out(p, 4)
                            if j == 1 and s == 0 and f2.exists:
                                expert_out(f2, 5)
                            if j == 3 and s < 15:
                                for f, k in work:
                                    if k > 0:
                                        expert_out(f, k - 1)
                        for u in tiles[1:]:
                            max_unit(owner, u)
                    if s == 10 and f2.exists:
                        expert_out(f2, BLOCKS - 1)
                    if s == 10 and t.plus(2).exists:
                        transpose_h(t.plus(2))
                    if s == 11 and f2.exists:
                        transpose_ffn(f2)
                    if s == 0 and n.exists:
                        project_v(n)
                    if p.exists:
                        if s == 2:
                            transpose_o2(p)
                        if s == 3:
                            project_o(p)
                        if s == 5:
                            transpose_xn2(p)
                        if s == 6:
                            route(p)
                        if s == 9:
                            transpose_comb(p)
                    if s in (12, 13) and t.plus(2).exists:
                        project_qk(t.plus(2), s - 12)

            def start_loop(t):
                blocks_done = BLOCKS * (t.n - 2) + 7
                assert last_reader[:2] == [(silu_done, BLOCKS * (t.first - 2) + 7), (up_copied, BLOCKS * (t.first - 2) + 7)]
                last_reader[:2] = [(silu_done, blocks_done), (up_copied, blocks_done)]

            def end_loop(t):
                assert [done for done, _ in last_reader[:2]] == [silu_done, up_copied]
                last_reader[:2] = [(done, BLOCKS * (t.n - 2) + 7) for done in (silu_done, up_copied)]

            run_iterations(pe, iteration, start_loop, end_loop)

        @block.scalar
        def _(act):
            def split_hi(ready, value, bank, dst, done, bias=None):
                act.wait_ge(ready, at(value))
                if bias is None:
                    nc.scalar.activation(dst, shared[:, bank], ACT.Copy).then_inc(done, 1)
                else:
                    nc.scalar.activation(dst, shared[:, bank], ACT.Identity, bias=bias).then_inc(done, 1)

            def split_h(n):
                if n.first > 0:
                    act.wait_ge(v_ready, at(n.n))
                split_hi(hT_ready, n.n + 1, 1, hT_hi[:], hT_hi_ready)

            def split_qk(n, side):
                wait(act, qk_stored, 64 * n.n)
                split_hi(qk_ready, 2 * n.n + side + 1, 1, qk_parts[:, side, 0], qk_hi_ready,
                         bias=qk_bias[:, side:side + 1])

            def copy_max(n, part):
                wait(act, max_stored[part], 16 * earlier(n, part))
                act.wait_ge(maxT_ready[part], at(earlier(n, part) + 1))
                nc.scalar.activation(maxT[part], shared[0:8 * len(MAX_PARTS[part]), 0], ACT.Copy)\
                    .then_inc(maxT_copied[part], 1)

            def load_x(n):
                act.wait_ge(xn_ready, at(n.n - 1))
                act.wait_ge(x_beta_ready, at(n.n - 1))
                act.dma_start(x_in[:, n.par], x_view[at(n.n)]).then_inc(x_loaded[n.par], 16)

            def exp_unit(b, u):
                act.wait_ge(scores_ready, at(UNITS * b.n + u + 1))
                if b.first == 0 and u == 0:
                    act.wait_ge(experts_split, 2)
                wait(act, pv_done, SETS * b.n + u // 4 - 1)
                nc.scalar.activation(probs[:, u % 8], exp_bank[:, u % 2], ACT.Exp,
                                     scale=float(DH) ** -0.5).then_inc(exp_done, 1)

            def copy_o(b, g):
                act.wait_ge(pv_done, at(SETS * b.n + TT * g + TT))
                wait(act, oq_ready, GROUPS * b.n + g - 1)
                nc.scalar.activation(oT[:, g % 2], out_bank[:], ACT.Copy).then_inc(oT_copied, 1)

            def exp_logits(b):
                act.wait_ge(logits_ready, at(b.n + 1))
                wait(act, route_step, ROUTE_STEPS * b.n)
                nc.scalar.activation(r_exp[:].rearrange("p t e -> p (t e)"), shared[:, 1, 0:TT * E], ACT.Exp,
                                     scale=-1.0).then_inc(logits_exp, 1)

            def copy_comb(b):
                act.wait_ge(combT_ready, at(b.n + 1))
                wait(act, comb_stored, 16 * b.n)
                nc.scalar.activation(combT[:], shared[0:E, 1], ACT.Copy).then_inc(combT_copied, 1)

            def gate_tanh(f, k, tail):
                act.wait_ge(gate_ready, at(BLOCKS * f.n + k + 1))
                wait(act, silu_done, BLOCKS * f.n + k - 1)
                nc.scalar.activation(f_tanh[:, (k + f.par) % 2], expert_banks(f, k, 0, tail)[1],
                                     ACT.Tanh, scale=0.5).then_inc(tanh_done, 1)

            def copy_up(f, k, tail):
                if tail and k > 0:
                    return
                act.wait_ge(up_ready, at(BLOCKS * f.n + k + 1))
                wait(act, act_done, BLOCKS * f.n + k - 1)
                nc.scalar.activation(f_up[:, (k + f.par) % 2], expert_banks(f, k, 1, tail)[1], ACT.Copy)\
                    .then_inc(up_copied, 1)

            def copy_ffn(f):
                act.wait_ge(down_done, at(BLOCKS * (f.n + 1)))
                wait(act, ffn_ready, f.n)
                nc.scalar.activation(ffnT[:], down_bank[:], ACT.Copy).then_inc(ffnT_copied, 1)

            act.wait_ge(weights_loaded, 64)
            act.wait_ge(consts_loaded, N_CONSTS)
            nc.scalar.activation(w_hi[:], w_raw[:], ACT.Copy).then_inc(w_hi_ready, 1)
            nc.scalar.activation(gate_hi[:], gate_raw[:], ACT.Copy).then_inc(w_hi_ready, 1)
            split_h(Batch(0))
            split_qk(Batch(0), 0)
            split_qk(Batch(0), 1)
            act.wait_ge(experts_loaded, 32)
            for side in range(2):
                nc.scalar.activation(wgu_hi[:, side].rearrange("p k m -> p (k m)"), raw_experts[side], ACT.Copy)\
                    .then_inc(experts_hi, 1)
            act.wait_ge(down_loaded, 16)
            nc.scalar.activation(w_down[:, 0], w_down[:, 0], ACT.Copy, scale=0.5).then_inc(down_loaded, 1)
            copy_max(Batch(0), 2)
            split_h(Batch(1))
            split_qk(Batch(1), 0)
            split_qk(Batch(1), 1)
            copy_max(Batch(0), 3)

            def iteration(t):
                b, n, p, f2 = t, t.plus(1), t.plus(-1), t.plus(-2)
                tail = t.first >= B
                for s in range(SLOTS):
                    if s == 0 and t.plus(2).exists:
                        load_x(t.plus(2))
                    if s == 11 and t.plus(2).exists:
                        split_h(t.plus(2))
                    if s in (13, 14) and t.plus(2).exists:
                        split_qk(t.plus(2), s - 13)
                    if s in (5, 9, 13) and b.exists:
                        copy_o(b, (s - 5) // 4)
                    if p.exists:
                        if s == 1:
                            copy_o(p, GROUPS - 1)
                        if s == 3:
                            split_hi(o2T_ready, p.n + 1, 1, o2T_hi[:], o2T_hi_ready)
                        if s == 6:
                            split_hi(xn2T_ready, p.n + 1, 1, xn2T_hi[:, p.par], xn2T_hi_ready)
                        if s == 7:
                            exp_logits(p)
                        if s == 10:
                            copy_comb(p)
                    if s == 11 and f2.exists:
                        copy_ffn(f2)
                    work = [(t.plus(-back), k) for k, back in FFN_SLOTS[s] if t.plus(-back).exists]
                    for j in range(4):
                        if b.exists:
                            exp_unit(b, 4 * s + j)
                        if j in (0, 2) and j // 2 < len(work):
                            gate_tanh(*work[j // 2], tail)
                        if j in (1, 3) and len(work) == 2:
                            copy_up(*work[j // 2], tail)
                        if j == 2 and len(work) == 1:
                            copy_up(*work[0], tail)
                        if (s, j) == (14, 3) and n.exists:
                            copy_max(n, 0)
                        for _, slot, part in max_slots(b):
                            if (s, j) == (slot, 3):
                                copy_max(b, part)

            run_iterations(act, iteration)

        @block.vector
        def _(dve):
            def settle(ins, done, value):
                ins.then_inc(done, 1)
                dve.wait_ge(done, at(value))

            def split_lo(hi_ready, value, bank, hi, lo, done, bias=None):
                dve.wait_ge(hi_ready, at(value))
                if bias is None:
                    ins = nc.vector.tensor_tensor(lo, shared[:, bank], hi.bitcast(F32), ALU.subtract)
                else:
                    ins = nc.vector.scalar_tensor_tensor(out=lo, in0=shared[:, bank], scalar=bias, in1=hi.bitcast(F32),
                                                         op0=ALU.add, op1=ALU.subtract)
                ins.then_inc(done, 1)

            def norm_stats(which, n, src):
                step = ln_step[which]
                for tt in range(TT):
                    nc.vector.bn_stats(stats[:, which, tt], src[:, tt])
                dve.drain()
                for tt in range(TT):
                    ins = nc.vector.bn_aggr(moments[:, which, tt], stats[:, which, tt])
                settle(ins, step, n.n + 1)
                nc.vector.tensor_scalar(var_eps[:, which], moments[:, which, :, 1], EPS, None, ALU.add)\
                    .then_inc(var_ready[which], 1)

            def norm_apply(which, n, src, dst, done):
                dve.wait_ge(rstd_ready[which], at(n.n + 1))
                for tt in range(TT):
                    ins = nc.vector.tensor_scalar(dst[:, tt], src[:, tt], moments[:, which, tt, 0:1],
                                                  rstd[:, which, tt:tt + 1], ALU.subtract, ALU.mult)
                ins.then_inc(done, 1)

            def norm_x(n, step):
                if step == 0:
                    dve.wait_ge(x_loaded[n.par], at(16 * (n.pair + 1)))
                    norm_stats(LN1, n, x_in[:, n.par])
                else:
                    wait(dve, h_ready, n.n)
                    norm_apply(LN1, n, x_in[:, n.par], xn, xn_ready)

            def split_h(n):
                split_lo(hT_hi_ready, n.n + 1, 1, hT_hi[:], hT_lo[:], hT_split)

            def split_qk(n, side):
                wait(dve, qk_stored, 64 * n.n)
                split_lo(qk_hi_ready, 2 * n.n + side + 1, 1, qk_parts[:, side, 0], qk_parts[:, side, 1],
                         qk_lo_ready, bias=qk_bias[:, side:side + 1])

            def copy_v(n):
                dve.wait_ge(v_ready, at(n.n + 1))
                if n.first >= 2:
                    dve.wait_ge(pv_done, at(SETS * (n.n - 1)))
                nc.vector.tensor_tensor(values[n.par][:, :, :, 0:DH],
                                        shared[:, 1].rearrange("p (t h d) -> p t h d", t=TT, h=H),
                                        bv_row[:].rearrange("p (h d) -> p h d", h=H).unsqueeze(1)
                                        .broadcast_to([P, TT, H, DH]), ALU.add)\
                    .then_inc(values_ready, 1)

            def take_max(n, u):
                g, qt, i = u // (4 * TT), (u // 4) % TT, u % 4
                if u == 0:
                    wait(dve, max_split[1], n.n)
                    if n.first == 1:
                        dve.wait_ge(max_split[4], 1)
                dve.wait_ge(max_scores, at(UNITS * n.n + u + 1))
                nc.vector.tensor_reduce(neg_max[:, qt, g, i:i + 1], max_bank[:, u % 2], AX_X, ALU.max,
                                        negate=True).then_inc(max_taken, 1)

            def split_max(n, part):
                groups = slice(MAX_PARTS[part].start, MAX_PARTS[part].stop)
                dve.wait_ge(max_taken, at(UNITS * n.n + 4 * TT * groups.stop))
                if n.first == 1 and part == 0:
                    for first_part in FIRST_PARTS[:-1]:
                        dve.wait_ge(maxT_ready[first_part], 1)
                wait(dve, maxT_ready[part], earlier(n, part))
                settle(nc.vector.tensor_copy(max_parts[:, :, groups, :, 0].bitcast(F32R), neg_max[:, :, groups]),
                       max_hi[part], earlier(n, part) + 1)
                nc.vector.tensor_tensor(max_parts[:, :, groups, :, 1].bitcast(F32R), neg_max[:, :, groups],
                                        max_parts[:, :, groups, :, 0], ALU.subtract).then_inc(max_split[part], 1)

            def normalise_o(b, g):
                dve.wait_ge(oq_ready, at(GROUPS * b.n + g + 1))
                wait(dve, o_ready, GROUPS * b.n + g - 1)
                heads = shared[:, 0].rearrange("p (t i c) -> p t i c", t=TT, i=4)
                settle(nc.vector.reciprocal(o_rcp[:, g % 2], heads[:, :, :, DH]), o_rcp_ready, GROUPS * b.n + g + 1)
                if g == 0:
                    wait(dve, o2T_ready, b.n)
                nc.vector.tensor_tensor(o[:].rearrange("p t (i g d) -> p t i g d", i=4, g=GROUPS)[:, :, :, g],
                                        heads[:, :, :, 0:DH],
                                        o_rcp[:, g % 2].unsqueeze(3).broadcast_to([P, TT, 4, DH]), ALU.mult)\
                    .then_inc(o_ready, 1)

            def residual(b):
                dve.wait_ge(wo_ready, at(b.n + 1))
                wait(dve, xn2T_ready, b.n)
                dve.wait_ge(h_ready, at(b.n + 1))
                dve.wait_ge(x_beta_ready, at(b.n + 1))
                ins = nc.vector.tensor_tensor(y[:], shared[:, 1].rearrange("p (t d) -> p t d", t=TT),
                                              h_bo[:, b.par], ALU.add)
                settle(ins, y_ready, b.n + 1)
                norm_stats(LN2, b, y)

            def finish_attention(b):
                if b.first >= 2:
                    dve.wait_ge(result_stored, at(16 * (b.n - 1)))
                for tt in range(TT):
                    ins = nc.vector.scalar_tensor_tensor(out=x2[:, b.par, tt], in0=y[:, tt],
                                                         scalar=moments[:, LN2, tt, 0:1], in1=gamma_row[:],
                                                         op0=ALU.subtract, op1=ALU.mult)
                settle(ins, yn_ready, b.n + 1)
                dve.wait_ge(rstd_ready[LN2], at(b.n + 1))
                for tt in range(TT):
                    ins = nc.vector.scalar_tensor_tensor(out=x2[:, b.par, tt], in0=x2[:, b.par, tt],
                                                         scalar=rstd[:, LN2, tt:tt + 1], in1=x_beta[:, b.par, tt],
                                                         op0=ALU.mult, op1=ALU.add)
                settle(ins, x2_step, b.n + 1)

            def norm_x2(b, step):
                if step == 0:
                    norm_stats(LN3, b, x2[:, b.par])
                else:
                    norm_apply(LN3, b, x2[:, b.par], y, xn2_ready)

            def score_groups(b):
                st = ROUTE_STEPS * b.n
                dve.wait_ge(logits_exp, at(b.n + 1))
                settle(nc.vector.tensor_scalar(r_den[:], r_exp[:], 1.0, None, ALU.add), route_step, st + 1)
                settle(nc.vector.reciprocal(r_sig[:], r_den[:]), route_step, st + 2)
                settle(nc.vector.tensor_tensor(r_sc[:], r_sig[:], route_bias[:].unsqueeze(1)
                                               .broadcast_to([P, TT, E]), ALU.add), route_step, st + 3)
                fours = r_sc[:].rearrange("p t (g a c) -> p (t g) a c", a=2, c=2)
                nc.vector.tensor_tensor(r_max[:], fours[:, :, :, 0], fours[:, :, :, 1], ALU.max).then_inc(route_step, 1)
                nc.vector.tensor_tensor(r_min[:], fours[:, :, :, 0], fours[:, :, :, 1], ALU.min).then_inc(route_step, 1)
                dve.wait_ge(route_step, at(st + 5))
                nc.vector.tensor_tensor(r_own[:], r_max[:], r_min[:], ALU.add).then_inc(route_step, 1)
                nc.vector.tensor_tensor(r_two[:, :, 0], r_max[:, :, 0], r_max[:, :, 1], ALU.add).then_inc(route_step, 1)
                dve.wait_ge(route_step, at(st + 7))
                settle(nc.vector.tensor_tensor(r_two[:, :, 1], r_own[:, :, 0], r_own[:, :, 1], ALU.max), route_step, st + 8)
                nc.vector.tensor_tensor(r_grp[:].rearrange("p t g -> p (t g)"), r_two[:, :, 0], r_two[:, :, 1],
                                        ALU.max).then_inc(route_step, 1)

            def open_groups(b):
                st = ROUTE_STEPS * b.n
                dve.drain()
                for tt in range(TT):
                    nc.vector.max(r_ranked[:, tt], r_grp[:, tt])
                dve.drain()
                nc.vector.tensor_copy(r_best[:, :, 0:4], r_ranked[:, :, 0:4]).then_inc(route_step, 1)
                dve.drain()
                for tt in range(TT):
                    nc.vector.match_replace(r_closed[:, tt], r_best[:, tt], r_grp[:, tt], -3.0e38)
                dve.drain()
                settle(nc.vector.tensor_tensor(r_open[:], r_closed[:], r_grp[:], ALU.not_equal), route_step, st + 11)

            def route_experts(b):
                group = lambda a: a[:].rearrange("p t (g e) -> p (t g) e", g=EG)
                nc.vector.tensor_tensor(group(r_masked), group(r_sc),
                                               r_open[:].rearrange("p t g -> p (t g)").unsqueeze(2)
                                               .broadcast_to([P, TT * EG, E // EG]), ALU.mult).then_inc(route_step, 1)
                dve.drain()
                for tt in range(TT):
                    nc.vector.max(r_top[:, tt], r_masked[:, tt])
                dve.drain()
                for tt in range(TT):
                    nc.vector.match_replace(r_rest[:, tt], r_top[:, tt], r_masked[:, tt], -3.0e38)
                dve.drain()
                settle(nc.vector.tensor_tensor(r_sel[:], r_rest[:], r_masked[:], ALU.not_equal), comb_step, 5 * b.n + 1)
                settle(nc.vector.tensor_tensor(r_w[:], r_sel[:], r_sig[:], ALU.mult), comb_step, 5 * b.n + 2)
                settle(nc.vector.tensor_reduce(r_sum[:, 0], r_w[:], AX_X, ALU.add), comb_step, 5 * b.n + 3)
                settle(nc.vector.tensor_scalar(r_sum[:, 1], r_sum[:, 0], 1e-20, None, ALU.add), comb_step, 5 * b.n + 4)
                settle(nc.vector.reciprocal(r_sum[:, 2], r_sum[:, 1]), comb_step, 5 * b.n + 5)
                wait(dve, combT_ready, b.n)
                nc.vector.scalar_tensor_tensor(out=comb[:], in0=r_w[:], scalar=ROUTE_SCALE / 2,
                                               in1=r_sum[:, 2].unsqueeze(2).broadcast_to([P, TT, E]),
                                               op0=ALU.mult, op1=ALU.mult).then_inc(comb_ready, 1)

            def silu(f, k, tail):
                dve.wait_ge(tanh_done, at(BLOCKS * f.n + k + 1))
                slot = (k + f.par) % 2
                wait(dve, act_done, BLOCKS * f.n + k - 1)
                nc.vector.scalar_tensor_tensor(out=f_silu[:, slot], in0=f_tanh[:, slot], scalar=1.0,
                                               in1=expert_banks(f, k, 0, tail)[1], op0=ALU.add, op1=ALU.mult)\
                    .then_inc(silu_done, 1)

            def times_up(f, k):
                dve.wait_ge(up_ready, at(BLOCKS * f.n + k + 1))
                dve.wait_ge(silu_done, at(BLOCKS * f.n + k + 1))
                wait(dve, act_done, BLOCKS * f.n + k - 1)
                nc.vector.tensor_tensor(f_up[:, (k + f.par) % 2], f_silu[:, (k + f.par) % 2],
                                        expert_banks(f, k, 1, True)[1], ALU.mult).then_inc(up_copied, 1)

            def finish(f):
                dve.wait_ge(ffn_ready, at(f.n + 1))
                nc.vector.tensor_tensor(x2[:, f.par], shared[:, 1].rearrange("p (t d) -> p t d", t=TT), x2[:, f.par],
                                        ALU.add).then_inc(result_ready, 1)

            norm_x(Batch(0), 0)
            norm_x(Batch(0), 1)
            nc.vector.memset(out_bank[:], 0.0).then_inc(out_bank_set, 1)
            nc.vector.memset(r_best[:], 3.0e38).then_inc(best_filled, 1)
            dve.wait_ge(best_filled, 1)
            for i in range(2):
                nc.vector.memset(k_stack[i][:].bitcast(F32), 1.0).then_inc(ones_set, 1)
            dve.wait_ge(w_hi_ready, 2)
            nc.vector.tensor_tensor(w_lo[:], w_raw[:], w_hi[:].bitcast(F32), ALU.subtract).then_inc(w_split, 1)
            nc.vector.tensor_tensor(gate_lo[:], gate_raw[:], gate_hi[:].bitcast(F32), ALU.subtract).then_inc(w_split, 1)
            split_h(Batch(0))
            split_qk(Batch(0), 0)
            split_qk(Batch(0), 1)
            dve.wait_ge(values_set, 2)
            copy_v(Batch(0))
            for u in range(FIRST_TILES):
                take_max(Batch(0), u)
                if u in (3, 7):
                    norm_x(Batch(1), (u - 3) // 4)
                if u == 15:
                    split_max(Batch(0), 2)
                if u == 19:
                    split_h(Batch(1))
                if u in (23, 25):
                    split_qk(Batch(1), (u - 23) // 2)
            split_max(Batch(0), 3)

            def iteration(t):
                n, p, f2 = t.plus(1), t.plus(-1), t.plus(-2)
                b, q = t, t.plus(2)
                tail = t.first >= B
                for s in range(SLOTS):
                    if s == 1 and n.exists:
                        copy_v(n)
                    if s == 11 and q.exists:
                        split_h(q)
                    if s in (13, 14) and q.exists:
                        split_qk(q, s - 13)
                    if p.exists:
                        if s == 3:
                            split_lo(o2T_hi_ready, p.n + 1, 1, o2T_hi[:], o2T_lo[:], o2T_split)
                        if s == 4:
                            residual(p)
                        if s == 5:
                            norm_x2(p, 0)
                        if s == 6:
                            split_lo(xn2T_hi_ready, p.n + 1, 1, xn2T_hi[:, p.par], xn2T_lo[:, p.par], xn2T_split)
                    if s == 12 and f2.exists:
                        finish(f2)
                    if s == 14 and n.exists:
                        split_max(n, 0)
                    for slot, _, part in max_slots(b):
                        if s == slot:
                            split_max(b, part)
                    work = [(t.plus(-back), k) for k, back in FFN_SLOTS[s] if t.plus(-back).exists]
                    for j in range(4):
                        if s in (5, 9, 13) and j == 3 and b.exists:
                            normalise_o(b, (s - 5) // 4)
                        if (s, j) == (1, 3) and p.exists:
                            normalise_o(p, GROUPS - 1)
                        owner, tiles = max_tiles(t, s, j)
                        for u in tiles[:1]:
                            take_max(owner, u)
                        if j in (1, 3) and j // 2 < len(work):
                            silu(*work[j // 2], tail)
                        if tail and (j == 2 and len(work) == 1 or j in (1, 3) and len(work) == 2):
                            f, k = work[j // 2 if len(work) == 2 else 0]
                            if k > 0:
                                times_up(f, k)
                        for u in tiles[1:]:
                            take_max(owner, u)
                        if p.exists:
                            if (s, j) == (7, 0):
                                score_groups(p)
                            if (s, j) == (7, 2):
                                open_groups(p)
                            if (s, j) == (8, 1):
                                route_experts(p)
                        if (s, j) == (4, 1) and p.exists:
                            finish_attention(p)
                        if (s, j) == (5, 1) and p.exists:
                            norm_x2(p, 1)
                        if (s, j) in ((1, 1), (1, 3)) and q.exists:
                            norm_x(q, j // 2)

            run_iterations(dve, iteration)

        @block.gpsimd
        def _(pool):
            def power(which, n):
                pool.wait_ge(var_ready[which], at(n.n + 1))
                wait(pool, (xn_ready, x2_step, xn2_ready)[which], n.n)
                nc.gpsimd.tensor_tensor(rstd[:, which], var_eps[:, which], minus_half[:], ALU.pow)\
                    .then_inc(rstd_ready[which], 1)

            def add_positions(n):
                pool.wait_ge(xn_ready, at(n.n + 1))
                wait(pool, hT_ready, n.n)
                wait(pool, x_beta_ready, n.n)
                nc.gpsimd.tensor_tensor(h[:], xn[:], pos[:], ALU.add).then_inc(h_ready, 1)

            def add_biases(n):
                pool.wait_ge(h_ready, at(n.n + 1))
                if n.first >= 2:
                    pool.wait_ge(x2_step, at(n.n - 1))
                row = lambda a: a[:].unsqueeze(1).broadcast_to([P, TT, P])
                nc.gpsimd.tensor_tensor(h_bo[:, n.par], h[:], row(bo_row), ALU.add).then_inc(h_bo_ready, 1)
                nc.gpsimd.tensor_tensor(x_beta[:, n.par], x_in[:, n.par], row(beta_row), ALU.add)\
                    .then_inc(x_beta_ready, 1)

            def gated_products(f, k, tail):
                up = f_up[:, (k + f.par) % 2]
                pool.wait_ge(up_copied, at(BLOCKS * f.n + k + 1))
                if k > 0 and (k - 1) % 4 == 0:
                    pool.wait_ge(comb_loaded[(k - 1) // 4], at(32 * (f.n + 1)))
                act_free = BLOCKS * f.n + k - 2 if k > 3 else BLOCKS * f.n if k else BLOCKS * (f.n - 1) + 1
                if tail and k > 0:
                    wait(pool, down_done, act_free)
                    nc.gpsimd.tensor_tensor(f_act[:, 1 + k % 3], up, comb_all[:, (k - 1) % 8], ALU.mult)\
                        .then_inc(act_done, 1)
                    return
                if k > 0:
                    nc.gpsimd.tensor_tensor(up, up, comb_all[:, (k - 1) % 8], ALU.mult).then_inc(weighed, 1)
                    pool.wait_ge(weighed, at((BLOCKS - 1) * f.n + k))
                pool.wait_ge(silu_done, at(BLOCKS * f.n + k + 1))
                wait(pool, down_done, act_free)
                nc.gpsimd.tensor_tensor(f_act[:, 1 + k % 3 if k else 0], f_silu[:, (k + f.par) % 2], up, ALU.mult)\
                    .then_inc(act_done, 1)

            nc.gpsimd.memset(minus_half[:], -0.5).then_inc(exponent_set, 1)
            pool.wait_ge(exponent_set, 1)
            power(LN1, Batch(0))
            for i in range(2):
                nc.gpsimd.memset(values[i][:, :, :, DH:DH + 1], 1.0).then_inc(values_set, 1)
            pool.wait_ge(consts_loaded, N_CONSTS)
            add_positions(Batch(0))
            add_biases(Batch(0))
            pool.wait_ge(experts_hi, 2)
            for side in range(2):
                nc.gpsimd.tensor_tensor(wgu_lo[:, side].rearrange("p k m -> p (k m)"), raw_experts[side],
                                        wgu_hi[:, side].rearrange("p k m -> p (k m)").bitcast(F32), ALU.subtract)\
                    .then_inc(experts_split, 1)
            power(LN1, Batch(1))
            add_positions(Batch(1))

            def iteration(t):
                n, p = t.plus(1), t.plus(-1)
                for s in range(SLOTS):
                    if s == 4 and p.exists:
                        power(LN2, p)
                    if s == 5 and p.exists:
                        power(LN3, p)
                    if s == 6 and n.exists:
                        add_biases(n)
                    if s == 1 and t.plus(2).exists:
                        power(LN1, t.plus(2))
                    if s == 8 and t.plus(2).exists:
                        add_positions(t.plus(2))
                    for k, back in FFN_SLOTS[s]:
                        f = t.plus(-back)
                        if f.exists:
                            gated_products(f, k, t.first >= B)

            run_iterations(pool, iteration)


def positional_encoding():
    import numpy as np

    position = np.arange(T, dtype=np.float32)[:, None]
    rate = np.exp(np.arange(0, P, 2, dtype=np.float32) * np.float32(-np.log(10000.0) / P)).astype(np.float32)
    table = np.zeros((T, P), np.float32)
    table[:, 0::2] = np.sin(position * rate)
    table[:, 1::2] = np.cos(position * rate)
    return table


def kernel(**inputs):
    import numpy as np
    import concourse.bacc as bacc
    from concourse import mybir as mb
    from concourse.bass_utils import run_bass_kernel_spmd

    a = {k: np.asarray(v) for k, v in inputs.items()}
    attn = lambda k: a[f"L0_attn_{k}"]
    ffn = lambda k: a[f"L0_ffn_{k}"]
    gate_in = np.concatenate([ffn("sh_gate").T, ffn("w_gate").reshape(E * EI, P).T], axis=1)
    up_in = np.concatenate([ffn("sh_up").T, ffn("w_up").reshape(E * EI, P).T], axis=1)
    down = np.concatenate([ffn("sh_down").T, ffn("w_down").transpose(0, 2, 1).reshape(E * EI, P)], axis=0)
    arrays = {
        "x": attn("x"), "wq": attn("Wq"), "wk": attn("Wk"), "wv": attn("Wv"), "wo": attn("Wo"),
        "bq": attn("bq"), "bk": attn("bk"), "bv": attn("bv"), "bo": attn("bo"),
        "gamma": attn("gamma"), "beta": attn("beta"),
        "gate_wT": ffn("gate_w").T, "gate_bias": ffn("gate_bias"),
        "w_gateT": gate_in, "w_upT": up_in,
        "w_downT": down.reshape(BLOCKS, P, P).transpose(1, 0, 2),
        "pe_table": positional_encoding().reshape(TT, P, P).transpose(1, 0, 2),
        "identity": np.eye(P, dtype=np.float32),
    }
    nc = bacc.Bacc("TRN2", target_bir_lowering=False, num_devices=1)
    arrays = {f"in_{k}": np.ascontiguousarray(v) for k, v in arrays.items()}
    args = [nc.dram_tensor(k, v.shape, mb.dt.from_np(v.dtype), kind="ExternalInput").ap() for k, v in arrays.items()]
    out = nc.dram_tensor("out_y", (B, T, P), mb.dt.float32, kind="ExternalOutput").ap()
    build_layer(nc, *args, out)
    r = run_bass_kernel_spmd(nc, [arrays], core_ids=[0])
    return r.results[0]["out_y"]
```
